# Optimizing a Trainium2 kernel written in Bass

```python
import numpy as np
import jax
import jax.numpy as jnp

def _softmax(x, axis=-1):
    return jax.nn.softmax(x, axis=axis)

def _gelu(x):
    return jax.nn.gelu(x, approximate=True)

def _silu(x):
    return jax.nn.silu(x)

def _sigmoid(x):
    return jax.nn.sigmoid(x)

def _layernorm(x, axis=-1, eps=1e-05):
    m = jnp.mean(x, axis=axis, keepdims=True)
    v = jnp.var(x, axis=axis, keepdims=True)
    return (x - m) / jnp.sqrt(v + eps)

def _scatter_add(tgt, idx, src, axis=0):
    return tgt.at[idx].add(src)

def _segment_sum(src, seg, n):
    return jax.ops.segment_sum(src, seg, n)
kernel_name = 'mk_gnn_resnorm_d2_gnn_r32_b55eda'

def setup_inputs(seed: int=0):
    np.random.seed(seed)
    _w = jnp.asarray

    def _rec_inputs():
        import jax
        import jax.numpy as jnp
        _gk = jax.random.key(seed)
        x = -0.0004942 + 1 * jax.random.normal(jax.random.fold_in(_gk, 1), (30000, 128), jnp.float32)
        src = jax.random.randint(jax.random.fold_in(_gk, 2), (30000,), 0, 30000, jnp.int32)
        dst = jnp.minimum((30000 * jax.random.uniform(jax.random.fold_in(_gk, 3), (30000,)) ** 2.0).astype(jnp.int32), 29999)
        _o = jnp.argsort(dst, stable=True)
        src = src[_o]
        dst = dst[_o]
        node_vec1 = jax.random.uniform(jax.random.fold_in(_gk, 13), (30000, 1), jnp.float32, 0.0, 0.999994)
        return (x, src, dst, node_vec1)
    x, src, dst, node_vec1 = _rec_inputs()

    def _L0_gnn_setup():
        import jax, jax.numpy as jnp
        import numpy as np
        N = 30000
        E = 15000
        D_IN = 128
        D_OUT = 128
        EPS = 1e-05
        key = jax.random.key(seed)
        ks = jax.random.split(key, 5)
        h = jax.random.normal(ks[0], (N, D_IN), jnp.float32)
        snorm_n = jax.random.uniform(ks[1], (N, 1), jnp.float32)
        W_fc = jax.random.normal(ks[2], (D_OUT, D_IN), jnp.float32) / np.sqrt(D_IN)
        gamma = jnp.ones((D_OUT,), jnp.float32)
        beta = jnp.zeros((D_OUT,), jnp.float32)
        src = jax.random.randint(ks[3], (E,), 0, N, dtype=jnp.int32)
        dst = jax.random.randint(ks[4], (E,), 0, N, dtype=jnp.int32)
        return {'h': h, 'snorm_n': snorm_n, 'W_fc': W_fc, 'gamma': gamma, 'beta': beta, 'src': src, 'dst': dst}
    _L0_gnn_all = _L0_gnn_setup()
    _L0_gnn_in = {k: v for k, v in _L0_gnn_all.items() if k in ('W_fc', 'gamma', 'beta')}
    del _L0_gnn_all

    def _L1_gnn_setup():
        import jax, jax.numpy as jnp
        import numpy as np
        N_NODES = 50000
        N_EDGES = 25000
        H = 128
        LN_EPS = 1e-05
        key = jax.random.key(seed)
        ks = jax.random.split(key, 8)
        x = jax.random.normal(ks[0], (N_NODES, H), dtype=jnp.float32)
        edge_index = jax.random.randint(ks[1], (2, N_EDGES), 0, N_NODES, dtype=jnp.int64)
        W1 = jax.random.normal(ks[2], (2 * H, H), dtype=jnp.float32) * 0.02
        b1 = jnp.zeros((H,), dtype=jnp.float32)
        W2 = jax.random.normal(ks[3], (H, 1), dtype=jnp.float32) * 0.02
        b2 = jnp.zeros((1,), dtype=jnp.float32)
        gamma = jnp.ones((H,), dtype=jnp.float32)
        beta = jnp.zeros((H,), dtype=jnp.float32)
        return {'x': x, 'edge_index': edge_index, 'W1': W1, 'b1': b1, 'W2': W2, 'b2': b2, 'gamma': gamma, 'beta': beta}
    _L1_gnn_all = _L1_gnn_setup()
    _L1_gnn_in = {k: v for k, v in _L1_gnn_all.items() if k in ('W1', 'b1', 'W2', 'b2', 'gamma', 'beta')}
    del _L1_gnn_all
    return {'x': x, 'src': src, 'dst': dst, 'node_vec1': node_vec1, 'L0_gnn_W_fc': _L0_gnn_in['W_fc'], 'L0_gnn_gamma': _L0_gnn_in['gamma'], 'L0_gnn_beta': _L0_gnn_in['beta'], 'L1_gnn_W1': _L1_gnn_in['W1'], 'L1_gnn_b1': _L1_gnn_in['b1'], 'L1_gnn_W2': _L1_gnn_in['W2'], 'L1_gnn_b2': _L1_gnn_in['b2'], 'L1_gnn_gamma': _L1_gnn_in['gamma'], 'L1_gnn_beta': _L1_gnn_in['beta']}

def reference(x, src, dst, node_vec1, L0_gnn_W_fc, L0_gnn_gamma, L0_gnn_beta, L1_gnn_W1, L1_gnn_b1, L1_gnn_W2, L1_gnn_b2, L1_gnn_gamma, L1_gnn_beta):
    import jax
    import jax.numpy as jnp

    def _L0_gnn_ref(h, snorm_n, W_fc, gamma, beta, src, dst):
        import jax, jax.numpy as jnp
        import numpy as np
        N = 30000
        E = 15000
        D_IN = 128
        D_OUT = 128
        EPS = 1e-05
        z = h @ W_fc.T
        z_src = z[src]
        e = z_src * z[dst]
        m = jax.ops.segment_max(e, dst, num_segments=N)
        ex = jnp.exp(e - m[dst])
        denom = jax.ops.segment_sum(ex, dst, num_segments=N)
        alpha = ex / denom[dst]
        hout = jax.ops.segment_sum(alpha * z_src, dst, num_segments=N)
        hout = hout * snorm_n
        mu = jnp.mean(hout, axis=0)
        var = jnp.var(hout, axis=0)
        hout = (hout - mu) * jax.lax.rsqrt(var + EPS) * gamma + beta
        return jax.nn.elu(hout)

    def _L1_gnn_ref(x, edge_index, W1, b1, W2, b2, gamma, beta):
        import jax, jax.numpy as jnp
        import numpy as np
        N_NODES = 50000
        N_EDGES = 25000
        H = 128
        LN_EPS = 1e-05
        src = edge_index[0]
        tgt = edge_index[1]
        edge_feat = jnp.concatenate([x[src], x[tgt]], axis=1)
        h = jax.nn.relu(edge_feat @ W1 + b1)
        w = jax.nn.sigmoid(h @ W2 + b2)[:, 0]
        agg = jax.ops.segment_sum(w[:, None] * x[src], tgt, num_segments=x.shape[0])
        attended = x + agg
        mu = jnp.mean(attended, axis=-1, keepdims=True)
        var = jnp.mean(jnp.square(attended - mu), axis=-1, keepdims=True)
        out = (attended - mu) * jax.lax.rsqrt(var + LN_EPS) * gamma + beta
        return out
    edge_index = jnp.stack([src, dst])
    x = _layernorm(x + _L0_gnn_ref(x, node_vec1, L0_gnn_W_fc, L0_gnn_gamma, L0_gnn_beta, src, dst), axis=-1)
    x = _layernorm(x + _L1_gnn_ref(x, edge_index, L1_gnn_W1, L1_gnn_b1, L1_gnn_W2, L1_gnn_b2, L1_gnn_gamma, L1_gnn_beta), axis=-1)
    return x

_drawn_inputs = setup_inputs


def setup_inputs(seed=0):
    import zlib

    import numpy as np

    out = dict(_drawn_inputs(seed))
    spreads = {'L0_gnn_gamma': (1.0, 0.2),
     'L0_gnn_beta': (0.0, 0.1),
     'L1_gnn_b1': (0.0, 0.8),
     'L1_gnn_gamma': (1.0, 0.2),
     'L1_gnn_beta': (0.0, 0.1)}
    factors = {'L1_gnn_W1': 8.0, 'L1_gnn_W2': 8.0}
    for name, (base, spread) in spreads.items():
        noise = np.random.default_rng([zlib.crc32(name.encode()), seed]).standard_normal(out[name].shape)
        drawn = base * np.exp(spread * noise) if base else spread * noise
        out[name] = jnp.asarray(drawn.astype(out[name].dtype))
    for name, factor in factors.items():
        out[name] = (out[name] * factor).astype(out[name].dtype)
    return out
```

```python
from contextlib import ExitStack

import concourse.bass as bass
from concourse import mybir

F32 = mybir.dt.float32
BF16 = mybir.dt.bfloat16
I32 = mybir.dt.int32
ALU = mybir.AluOpType
ACT = mybir.ActivationFunctionType

P = 128
EPS = 1e-5
N_CONSTS = 12
BN_STEPS = 7
BANK_PAIR = [0, 2, 4, 6, 2]
ACT_NORM_FROM = 3
BIG = 1.6e38
PEELED = 2
ROWS = 125
TPC = 4
CHUNK = ROWS * TPC
ESLOTS = 3
NPART = 120
TPN = 5
NSLOTS = 5


def later(k, n):
    return not isinstance(k, int) or k >= n


def loop_steps(eng, count, slots, step):
    for k in range(PEELED * slots):
        step(k, k % slots, k // slots)
    with eng.Fori(PEELED, count // slots) as i:
        for u in range(slots):
            step(i * slots + u, u, i)


def loads_done(i):
    return 16 * (i + 1)


def gnn_two_layers(nc, x, src, dst, snorm, w_fc, gamma0, beta0, w1, b1, w2, b2, gamma1, beta1, out):
    N, D = x.shape
    E = src.shape[0]
    assert N == E and D == P and E % (CHUNK * ESLOTS) == 0
    EC = E // CHUNK
    ET = E // ROWS
    PER_PART = N // NPART
    NCH = PER_PART // TPN
    EROWS = E // NPART
    HALVES = EROWS // ROWS
    assert HALVES == 2 and NCH % NSLOTS == 0 and PER_PART * NPART == N

    keep_dram = nc.dram_tensor("keep_scratch", (E,), BF16, kind="Internal").ap()
    gate_dram = nc.dram_tensor("gate_scratch", (E,), BF16, kind="Internal").ap()
    hout_dram = nc.dram_tensor("hout_scratch", (N, D), F32, kind="Internal").ap()
    x1_dram = nc.dram_tensor("x1_scratch", (N, D), F32, kind="Internal").ap()
    agg_dram = nc.dram_tensor("agg_scratch", (N, D), F32, kind="Internal").ap()

    def node_chunk(table, c):
        return table.rearrange("(p j) f -> p j f", p=NPART)[:, bass.ds(c * TPN, TPN), :]

    with ExitStack() as ctx:
        def sb(name, shape, dt=F32):
            return ctx.enter_context(nc.sbuf_tensor(name, shape, dt))

        def sem(name):
            return ctx.enter_context(nc.semaphore(name))

        def sems(name, n):
            return [sem(f"{name}{i}") for i in range(n)]

        banks = [ctx.enter_context(nc.psum_tensor(f"bank{i}", [P, 512], F32)) for i in range(8)]

        nodes = sb("nodes", [NPART, PER_PART, D])
        ARENA = 16400
        arena = sb("arena", [P, ARENA])

        def carve(sizes):
            at, views = 0, []
            for n in sizes:
                views.append(arena[:, at:at + n])
                at += n
            assert at <= ARENA, at
            return views

        SRC, DST, END = range(3)
        idx_all = sb("idx_all", [P, EC + ESLOTS, 3, TPC], I32)
        idx_now = sb("idx_now", [P, ESLOTS, 3, TPC], I32)
        ident = sb("ident", [P, P])
        w_fc_sb = sb("w_fc_sb", [P, P])
        w_fcT = sb("w_fcT", [P, P])
        w1_sb = sb("w1_sb", [P, 2, P])
        w2_col = sb("w2_col", [P, 1])
        w2_wide = sb("w2_wide", [P, P])
        cols = sb("cols", [P, 16])
        b1_col, b2_col, g0_col, be0_col = (cols[:, i:i + 1] for i in range(4))
        eps_col, sd_col, rs_col, a_col, ma_col, b_col = (cols[:, i:i + 1] for i in range(4, 10))
        mv0 = cols[:, 10:12]
        g1_row = sb("g1_row", [NPART, D])
        be1_row = sb("be1_row", [NPART, D])
        a_row = sb("a_row", [NPART, D])
        b_row = sb("b_row", [NPART, D])
        snorm_sb = sb("snorm_sb", [NPART, PER_PART])

        A = carve([EROWS] * 9)
        src_i, dst_i, nxt_i, prv_i = (a[0:NPART].bitcast(I32) for a in A[0:4])
        src_f, dst_f, same_f, end_f = (a[0:NPART] for a in A[4:8])
        bf = A[8][0:NPART].bitcast(BF16)
        keep_b, gate_b = bf[:, 0:EROWS], bf[:, EROWS:2 * EROWS]
        ZER = 640
        V = carve([TPC * D] * 9 + [CHUNK] * 5 + [CHUNK + 1] * 3 + [CHUNK] * 9 + [CHUNK // 2] * 3 + [ZER])
        rows_s = [v.rearrange("p (t f) -> p t f", f=D) for v in V[0:3]]
        rows_d = [v.rearrange("p (t f) -> p t f", f=D) for v in V[3:6]]
        rows_y = [v.rearrange("p (t f) -> p t f", f=D) for v in V[6:9]]
        xsT, xdT, zsT, e_t, delta = V[9:14]
        gmax = V[14:17]
        c_t, ex_t = V[17:19]
        den, num, y_t = V[19:22], V[22:25], V[25]
        hid, att_w = V[12], V[13]
        msg = V[17]
        aggT = V[19:22]
        gate_t = [v.bitcast(BF16) for v in V[26:29]]
        zeros = V[29]
        NV = carve([TPN * D] * (4 * NSLOTS) + [PER_PART * 6] + [PER_PART] * 6)
        nview = [v[0:NPART].rearrange("p (j f) -> p j f", f=D) for v in NV[0:4 * NSLOTS]]
        nx, nv, ne, no = (nview[NSLOTS * i:NSLOTS * (i + 1)] for i in range(4))
        st1 = NV[20][0:NPART].rearrange("p (j s) -> p j s", s=6)
        m_s, m_d, v_s, v_q, rstd1, mb1 = (v[0:NPART] for v in NV[21:27])
        a_wide = sb("a_wide", [P, NPART])[:, :]
        b_wide = sb("b_wide", [P, NPART])[:, :]
        st0 = sb("st0", [P, 2 * NCH, 6])
        st2 = sb("st2", [NPART, NSLOTS, TPN, 6])
        mv2 = sb("mv2", [NPART, NSLOTS, TPN, 2])
        rs2 = sb("rs2", [NPART, NSLOTS, TPN])
        eps_n = sb("eps_n", [NPART, 1])

        consts = sem("consts")
        minus_one = sem("minus_one")
        shifted = sem("shifted")
        ident_zero = sem("ident_zero")
        ident_ready = sem("ident_ready")
        small = sem("small")
        tables = sem("tables")
        idx_turned = sem("idx_turned")
        idx_ready = sem("idx_ready")
        gates_stored = sem("gates_stored")
        zeros_ready = sem("zeros_ready")
        zeroed = sem("zeroed")

        block = ctx.enter_context(nc.Block())

        def edge_sems(n):
            return dict(
                gathered=sems(f"gathered{n}_", ESLOTS), gates=sems(f"gates{n}_", ESLOTS),
                scattered=sems(f"scattered{n}_", ESLOTS), staged=sem(f"staged{n}"),
                turned=sem(f"turned{n}"), copied=sem(f"copied{n}"), product=sem(f"product{n}"),
                zs_copied=sem(f"zs_copied{n}"), weight=sem(f"weight{n}"), y_turned=sem(f"y_turned{n}"),
                y_rows=sem(f"y_rows{n}"), y_ready=sem(f"y_ready{n}"), logit=sem(f"logit{n}"))
        L0, L1 = edge_sems(0), edge_sems(1)
        e_ready, carry_ready, gmax_ready, delta_ready = (sem(s) for s in ("e_ready", "carry_ready", "gmax_ready", "delta_ready"))
        act_step, exps_ready, w_ready, den_ready, num_ready = (sem(s) for s in ("act_step", "exps_ready", "w_ready", "den_ready", "num_ready"))
        rec_ready, ln_small = sem("rec_ready"), sem("ln_small")
        msg_ready = sem("msg_ready")
        hout_loaded = sems("hout_loaded", NSLOTS)
        kept = sem("kept")
        scaled, node_turned, stats0 = sem("scaled"), sem("node_turned"), sem("stats0")
        bn_step, bn_sqrt, ab_turned, ab_ready = sem("bn_step"), sem("bn_sqrt"), sem("ab_turned"), sem("ab_ready")
        x_loaded = sems("x_loaded", NSLOTS)
        va_ready, v_ready, neg_ready, elu_ready, t_ready, s_ready = (sem(s) for s in ("va_ready", "v_ready", "neg_ready", "elu_ready", "t_ready", "s_ready"))
        stats1, ln_step, ln_sqrt, norm_dve, norm_act = (sem(s) for s in ("stats1", "ln_step", "ln_sqrt", "norm_dve", "norm_act"))
        x1_stored = sem("x1_stored")
        agg_loaded = sems("agg_loaded", NSLOTS)
        out_stored = sems("out_stored", NSLOTS)
        n2 = {s: sem("n2_" + s) for s in ("att", "st", "mv", "sd", "rs", "xb", "t", "s", "stb", "mvb", "sdb", "rsb", "out")}

        @block.sync
        def _(sp):
            col = lambda v: v.rearrange("(p o) -> p o", o=1)
            loads = [(src_i, src.rearrange("(p j) -> p j", p=NPART)),
                     (dst_i, dst.rearrange("(p j) -> p j", p=NPART)),
                     (w_fc_sb[:, :], w_fc), (w1_sb[:, :, :], w1.rearrange("(a k) h -> k a h", a=2)),
                     (w2_col[:, :], w2), (b1_col, col(b1)), (b2_col, b2.partition_broadcast(P)),
                     (g0_col, col(gamma0)), (be0_col, col(beta0)),
                     (g1_row[:, :], gamma1.partition_broadcast(NPART)),
                     (be1_row[:, :], beta1.partition_broadcast(NPART)),
                     (snorm_sb[:, :], snorm.rearrange("(p j) o -> p (j o)", p=NPART))]
            assert len(loads) == N_CONSTS
            for to, fr in loads:
                sp.dma_start(to, fr).then_inc(consts, 16)
            sp.wait_ge(minus_one, 1)
            last = (NPART - 1) * EROWS
            sp.dma_start(nxt_i[0:NPART - 1, :], dst[1:last + 1].rearrange("(p j) -> p j", j=EROWS)).then_inc(shifted, 16)
            sp.dma_start(nxt_i[NPART - 1:NPART, 0:EROWS - 1], dst[last + 1:E].rearrange("(p j) -> p j", p=1)).then_inc(shifted, 16)
            sp.dma_start(prv_i[0:1, 1:EROWS], dst[0:EROWS - 1].rearrange("(p j) -> p j", p=1)).then_inc(shifted, 16)
            sp.dma_start(prv_i[1:NPART, :], dst[EROWS - 1:E - 1].rearrange("(p j) -> p j", j=EROWS)).then_inc(shifted, 16)
            sp.wait_ge(tables, 6)
            sp.dma_start(keep_dram.rearrange("(p j) -> p j", p=NPART), keep_b).then_inc(gates_stored, 16)
            sp.dma_start(gate_dram.rearrange("(p j) -> p j", p=NPART), gate_b).then_inc(gates_stored, 16)
            sp.wait_ge(zeros_ready, 1)
            def zero_rows(c):
                sp.dma_start(node_chunk(hout_dram, c), zeros[0:NPART].rearrange("p (j f) -> p j f", f=D)).then_inc(zeroed, 16)
                sp.dma_start(node_chunk(agg_dram, c), zeros[0:NPART].rearrange("p (j f) -> p j f", f=D)).then_inc(zeroed, 16)
            with sp.Fori(0, NCH) as c:
                zero_rows(c)
            sp.wait_ge(gates_stored, 32)

            def gate_load(L, table, used):
                def step(k, u, i):
                    if later(k, ESLOTS):
                        sp.wait_ge(used, k - ESLOTS + 1)
                    sp.dma_start(gate_t[u][:, 0:CHUNK], table[bass.ds(k * CHUNK, CHUNK)].partition_broadcast(P)).then_inc(L["gates"][u], 16)
                return step
            loop_steps(sp, EC, ESLOTS, gate_load(L0, gate_dram, gmax_ready))

            for u in range(ESLOTS):
                sp.wait_ge(L0["scattered"][u], 16 * TPC * (EC // ESLOTS))
            def hout_load(c, u, i):
                if later(c, NSLOTS):
                    sp.wait_ge(scaled, c - NSLOTS + 1)
                sp.dma_start(nx[u], node_chunk(hout_dram, c)).then_inc(hout_loaded[u], 16)
            loop_steps(sp, NCH, NSLOTS, hout_load)
            def x_load(c, u, i):
                if later(c, NSLOTS):
                    sp.wait_ge(s_ready, c - NSLOTS + 1)
                sp.dma_start(nx[u], node_chunk(x, c)).then_inc(x_loaded[u], 16)
            sp.wait_ge(scaled, NCH)
            loop_steps(sp, NCH, NSLOTS, x_load)
            with sp.Fori(0, NCH) as c:
                sp.wait_ge(norm_dve, c + 1)
                sp.wait_ge(norm_act, c + 1)
                sp.dma_start(node_chunk(x1_dram, c), nodes[:, bass.ds(c * TPN, TPN), :]).then_inc(x1_stored, 16)

            loop_steps(sp, EC, ESLOTS, gate_load(L1, keep_dram, L1["y_ready"]))

            for u in range(ESLOTS):
                sp.wait_ge(L1["scattered"][u], 16 * TPC * (EC // ESLOTS))
            def agg_load(c, u, i):
                if later(c, NSLOTS):
                    sp.wait_ge(n2["t"], c - NSLOTS + 1)
                sp.dma_start(nx[u], node_chunk(agg_dram, c)).then_inc(agg_loaded[u], 16)
            loop_steps(sp, NCH, NSLOTS, agg_load)
            for u in range(NSLOTS):
                sp.wait_ge(out_stored[u], 16 * (NCH // NSLOTS))

        @block.gpsimd
        def _(pool):
            pool.memset(nxt_i, -1)
            pool.memset(prv_i, -1).then_inc(minus_one, 1)
            pool.memset(zeros, 0.0).then_inc(zeros_ready, 1)
            pool.memset(ident[:, :], 0.0).then_inc(ident_zero, 1)
            pool.wait_ge(ident_zero, 1)
            pool.affine_select(out=ident[:, :], in_=ident[:, :], compare_op=ALU.not_equal, fill=1.0, base=0,
                               pattern=[[-1, P]], channel_multiplier=1).then_inc(ident_ready, 1)

            def gather(L, table, k, u, i):
                if later(k, ESLOTS):
                    pool.wait_ge(L["turned"], k - ESLOTS + 1)
                    pool.nop(nofuse=True)
                if later(k, 2 * ESLOTS):
                    pool.wait_ge(L["scattered"][u], (i - 1) * 16 * TPC)
                pool.tensor_copy(idx_now[0:ROWS, u, :, :],
                                 idx_all[0:ROWS, bass.ds(k, 1), :, :].rearrange("r o n t -> r (o n) t")).then_inc(L["staged"], 1)
                pool.wait_ge(L["staged"], k + 1)
                pool.nop(nofuse=True)
                for t in range(TPC):
                    for n, rows in ((SRC, rows_s), (DST, rows_d)):
                        pool.indirect_dma_start(
                            out=rows[u][0:ROWS, t, :], out_offset=None, in_=table,
                            in_offset=bass.IndirectOffsetOnAxis(ap=idx_now[0:ROWS, u, n, t:t + 1], axis=0),
                        ).then_inc(L["gathered"][u], 16)

            def scatter(L, table, k, u):
                pool.wait_ge(L["y_rows"], k + 1)
                pool.nop(nofuse=True)
                for t in range(TPC):
                    pool.indirect_dma_start(
                        out=table, out_offset=bass.IndirectOffsetOnAxis(ap=idx_now[0:ROWS, u, END, t:t + 1], axis=0),
                        in_=rows_y[u][0:ROWS, t, :], in_offset=None, bounds_check=N - 1, oob_is_err=False,
                    ).then_inc(L["scattered"][u], 16)

            def edge_pass(L, table, result):
                for k in range(PEELED * ESLOTS):
                    gather(L, table, k, k % ESLOTS, k // ESLOTS)
                    if k >= ESLOTS:
                        scatter(L, result, k - ESLOTS, k % ESLOTS)
                with pool.Fori(PEELED, EC // ESLOTS) as i:
                    for u in range(ESLOTS):
                        gather(L, table, i * ESLOTS + u, u, i)
                        scatter(L, result, i * ESLOTS + u - ESLOTS, u)
                for u in range(ESLOTS):
                    pool.wait_ge(L["scattered"][u], (EC // ESLOTS - 1) * 16 * TPC)
                    pool.tensor_copy(idx_now[0:ROWS, u, END, :], idx_all[0:ROWS, EC + u, END, :]).then_inc(L["staged"], 1)
                    pool.wait_ge(L["staged"], EC + u + 1)
                    scatter(L, result, EC - ESLOTS + u, u)

            pool.wait_ge(idx_ready, 3)
            pool.wait_ge(gates_stored, 32)
            pool.wait_ge(zeroed, 32 * NCH)
            edge_pass(L0, x, hout_dram)
            pool.wait_ge(x1_stored, 16 * NCH)
            edge_pass(L1, x1_dram, agg_dram)

        @block.tensor
        def _(pe):
            pe.wait_ge(ident_ready, 1)
            pe.wait_ge(consts, 16 * N_CONSTS)
            pe.wait_ge(tables, 3)
            for n, tab in enumerate((src_f, dst_f, end_f)):
                for h in range(HALVES):
                    mm = pe.transpose(banks[n][0:ROWS, h * NPART:(h + 1) * NPART],
                                      tab[:, h * ROWS:(h + 1) * ROWS], ident[0:NPART, 0:NPART])
                mm.then_inc(idx_turned, 1)
            pe.transpose(banks[3][:, 0:P], w_fc_sb[:, :], ident[:, :]).then_inc(idx_turned, 1)

            def turn(L, k, u, i):
                pe.wait_ge(L["gathered"][u], (i + 1) * 32 * TPC)
                if later(k, 1):
                    pe.wait_ge(L["copied"], k)
                for bank, rows in ((0, rows_s), (1, rows_d)):
                    for t in range(TPC):
                        mm = pe.transpose(banks[bank][:, t * ROWS:(t + 1) * ROWS], rows[u][0:ROWS, t, :], ident[0:ROWS, 0:ROWS])
                mm.then_inc(L["turned"], 1)

            def turn_back(L, k, ys):
                pe.wait_ge(L["y_ready"], k + 1)
                if later(k, 1):
                    pe.wait_ge(L["y_rows"], k)
                for t in range(TPC):
                    mm = pe.transpose(banks[4][0:ROWS, t * D:(t + 1) * D], ys[:, t * ROWS:(t + 1) * ROWS], ident[:, :])
                mm.then_inc(L["y_turned"], 1)

            def step0(k, u, i):
                turn(L0, k, u, i)
                pe.wait_ge(L0["copied"], k + 1)
                if later(k, 1):
                    pe.wait_ge(L0["zs_copied"], k)
                    pe.wait_ge(e_ready, k)
                pe.matmul(banks[2][:, 0:CHUNK], w_fcT[:, :], xsT, start=True, stop=True)
                pe.matmul(banks[3][:, 0:CHUNK], w_fcT[:, :], xdT, start=True, stop=True).then_inc(L0["product"], 1)
                if later(k, 1):
                    turn_back(L0, k - 1, y_t)
            pe.wait_ge(idx_ready, 4)
            loop_steps(pe, EC, ESLOTS, step0)
            turn_back(L0, EC - 1, y_t)

            def turn_nodes(c, u, i):
                pe.wait_ge(scaled, c + 1)
                if later(c, 2):
                    pe.wait_ge(stats0, c - 1)
                pair = BANK_PAIR[u]
                for j in range(TPN):
                    mm = pe.transpose(banks[pair + j // 3][:, (j % 3) * NPART:(j % 3 + 1) * NPART],
                                      nv[u][:, j, :], ident[0:NPART, 0:NPART])
                mm.then_inc(node_turned, 1)
            pe.wait_ge(L0["y_rows"], EC)
            loop_steps(pe, NCH, NSLOTS, turn_nodes)
            pe.wait_ge(bn_step, BN_STEPS)
            for bank, c in ((4, a_wide), (5, b_wide)):
                mm = pe.matmul(banks[bank][0:NPART, 0:D], c, ident[:, :], start=True, stop=True)
            mm.then_inc(ab_turned, 1)

            def step1(k, u, i):
                turn(L1, k, u, i)
                pe.wait_ge(L1["copied"], k + 1)
                if later(k, 1):
                    pe.wait_ge(L1["zs_copied"], k)
                pe.matmul(banks[2][:, 0:CHUNK], w1_sb[:, 0, :], xsT, start=True, stop=False)
                pe.matmul(banks[2][:, 0:CHUNK], w1_sb[:, 1, :], xdT, start=False, stop=True).then_inc(L1["product"], 1)
                if later(k, 1):
                    turn_back(L1, k - 1, aggT[(u - 1) % ESLOTS])
                pe.wait_ge(L1["zs_copied"], k + 1)
                if later(k, 1):
                    pe.wait_ge(L1["weight"], k)
                pe.matmul(banks[3][:, 0:CHUNK], w2_wide[:, :], hid, start=True, stop=True).then_inc(L1["logit"], 1)
            pe.wait_ge(ab_ready, 2)
            loop_steps(pe, EC, ESLOTS, step1)
            turn_back(L1, EC - 1, aggT[(EC - 1) % ESLOTS])

        @block.scalar
        def _(act):
            def copy_in(L, k, free, lag):
                act.wait_ge(L["turned"], k + 1)
                if later(k, lag):
                    act.wait_ge(free, k + 1 - lag)
                act.copy(xsT, banks[0][:, 0:CHUNK])
                act.copy(xdT, banks[1][:, 0:CHUNK]).then_inc(L["copied"], 1)

            def copy_rows(L, k, u, i):
                act.wait_ge(L["y_turned"], k + 1)
                if later(k, ESLOTS):
                    act.wait_ge(L["scattered"][u], i * 16 * TPC)
                act.copy(rows_y[u][0:ROWS], banks[4][0:ROWS, :].rearrange("p (t f) -> p t f", f=D)).then_inc(L["y_rows"], 1)

            def step0(k, u, i):
                copy_in(L0, k, L0["product"], 1)
                act.wait_ge(L0["product"], k + 1)
                if later(k, 1):
                    act.wait_ge(w_ready, k)
                act.copy(zsT, banks[2][:, 0:CHUNK]).then_inc(L0["zs_copied"], 1)
                if later(k, 1):
                    copy_rows(L0, k - 1, (u - 1) % ESLOTS, i if u else i - 1)
                act.wait_ge(delta_ready, k + 1)
                if later(k, 1):
                    act.wait_ge(num_ready, k)
                act.activation(c_t, delta, ACT.Relu).then_inc(act_step, 1)
                act.activation(ex_t, delta, ACT.Relu, scale=-1.0).then_inc(act_step, 1)
                act.wait_ge(act_step, 2 * k + 2)
                act.activation(c_t, c_t, ACT.Exp, scale=-1.0)
                act.activation(ex_t, ex_t, ACT.Exp, scale=-1.0).then_inc(exps_ready, 1)
            loop_steps(act, EC, ESLOTS, step0)
            copy_rows(L0, EC - 1, (EC - 1) % ESLOTS, EC // ESLOTS - 1)

            def keep_rows(c, u, i):
                act.wait_ge(scaled, c + 1)
                act.copy(nodes[:, bass.ds(c * TPN, TPN), :], nv[u]).then_inc(kept, 1)
            loop_steps(act, NCH, NSLOTS, keep_rows)
            act.wait_ge(bn_step, 1)
            act.activation(sd_col, mv0[:, 1:2], ACT.Sqrt, bias=eps_col).then_inc(bn_sqrt, 1)
            def elu(c, u, i):
                act.wait_ge(v_ready, c + 1)
                if later(c, NSLOTS):
                    act.wait_ge(t_ready, c - NSLOTS + 1)
                act.activation(ne[u], nv[u], ACT.Relu, scale=-1.0).then_inc(neg_ready, 1)
                act.wait_ge(neg_ready, c + 1)
                act.activation(ne[u], ne[u], ACT.Exp, scale=-1.0).then_inc(elu_ready, 1)
            loop_steps(act, NCH, NSLOTS, elu)
            act.wait_ge(ln_step, 3)
            act.activation(v_s, v_q, ACT.Sqrt, bias=eps_n[:, :]).then_inc(ln_sqrt, 1)
            act.wait_ge(ln_step, 5)
            with act.Fori(0, NCH) as c:
                for j in range(ACT_NORM_FROM, TPN):
                    row = nodes[:, bass.ds(c * TPN + j, 1), :].rearrange("p o f -> p (o f)")
                    a = act.activation(row, row, ACT.Identity, bias=mb1[:, bass.ds(c * TPN + j, 1)], scale=rstd1[:, bass.ds(c * TPN + j, 1)])
                a.then_inc(norm_act, 1)

            def step1(k, u, i):
                copy_in(L1, k, msg_ready, 1)
                act.wait_ge(L1["product"], k + 1)
                if later(k, 1):
                    act.wait_ge(L1["logit"], k)
                act.activation(hid, banks[2][:, 0:CHUNK], ACT.Relu, bias=b1_col).then_inc(L1["zs_copied"], 1)
                if later(k, 1):
                    copy_rows(L1, k - 1, (u - 1) % ESLOTS, i if u else i - 1)
                act.wait_ge(L1["logit"], k + 1)
                if later(k, 1):
                    act.wait_ge(msg_ready, k)
                act.activation(att_w, banks[3][:, 0:CHUNK], ACT.Sigmoid, bias=b2_col).then_inc(L1["weight"], 1)
            act.wait_ge(x1_stored, 16 * NCH)
            loop_steps(act, EC, ESLOTS, step1)
            copy_rows(L1, EC - 1, (EC - 1) % ESLOTS, EC // ESLOTS - 1)

            def roots(c, u, i):
                act.wait_ge(n2["mv"], c + 1)
                act.activation(rs2[:, u, :], mv2[:, u, :, 1:2].rearrange("p j o -> p (j o)"), ACT.Sqrt, bias=eps_n[:, :]).then_inc(n2["sd"], 1)
                act.wait_ge(n2["mvb"], c + 1)
                act.activation(rs2[:, u, :], mv2[:, u, :, 1:2].rearrange("p j o -> p (j o)"), ACT.Sqrt, bias=eps_n[:, :]).then_inc(n2["sdb"], 1)
                act.wait_ge(n2["out"], c + 1)
                act.dma_start(node_chunk(out, c), no[u]).then_inc(out_stored[u], 16)
            loop_steps(act, NCH, NSLOTS, roots)

        @block.vector
        def _(dve):
            dve.memset(idx_all[:, 0:ESLOTS, END, :], 0)
            dve.memset(eps_col, EPS)
            dve.memset(eps_n[:, :], EPS)
            dve.wait_ge(consts, 16 * N_CONSTS)
            dve.wait_ge(shifted, 64)
            dve.tensor_copy(src_f, src_i).then_inc(tables, 1)
            dve.tensor_copy(dst_f, dst_i).then_inc(tables, 1)
            dve.tensor_tensor(same_f, dst_i, nxt_i, ALU.is_equal).then_inc(small, 1)
            dve.wait_ge(small, 1)
            dve.wait_ge(tables, 2)
            dve.scalar_tensor_tensor(out=end_f, in0=same_f, scalar=float(N), in1=dst_f, op0=ALU.mult, op1=ALU.add).then_inc(tables, 1)
            dve.tensor_tensor(keep_b, dst_i, prv_i, ALU.is_equal).then_inc(tables, 1)
            dve.tensor_scalar(gate_b, same_f, 2 * BIG, -BIG, ALU.mult, ALU.add).then_inc(tables, 1)
            dve.tensor_copy(w2_wide[:, :], w2_col[:, 0:1].to_broadcast([P, P])).then_inc(tables, 1)
            for n, first in ((SRC, 0), (DST, 0), (END, ESLOTS)):
                dve.wait_ge(idx_turned, n + 1)
                for h in range(HALVES):
                    last = dve.tensor_copy(idx_all[0:ROWS, first:first + EC, n, h::HALVES],
                                           banks[n][0:ROWS, h * NPART:(h + 1) * NPART].rearrange("r (k t) -> r k t", k=EC))
                last.then_inc(idx_ready, 1)
            dve.wait_ge(idx_turned, 4)
            dve.tensor_copy(w_fcT[:, :], banks[3][:, 0:P]).then_inc(idx_ready, 1)
            dve.wait_ge(gates_stored, 32)
            dve.wait_ge(idx_ready, 4)
            dve.memset(gmax[0][:, 0:1], -BIG).then_inc(carry_ready, 1)

            def step0(k, u, i):
                dve.wait_ge(L0["zs_copied"], k + 1)
                dve.tensor_tensor(e_t, banks[3][:, 0:CHUNK], zsT, ALU.mult).then_inc(e_ready, 1)
                prev = gmax[(u - 1) % ESLOTS]
                first = not later(k, 1)
                if not first:
                    dve.wait_ge(gmax_ready, k)
                    dve.tensor_copy(gmax[u][:, 0:1], prev[:, CHUNK:CHUNK + 1]).then_inc(carry_ready, 1)
                dve.wait_ge(e_ready, k + 1)
                dve.wait_ge(L0["gates"][u], loads_done(i))
                dve.tensor_tensor_scan(gmax[u][:, 1:CHUNK + 1], e_t, gate_t[u][:, 0:CHUNK],
                                       -BIG if first else prev[:, CHUNK:CHUNK + 1], ALU.max, ALU.min).then_inc(gmax_ready, 1)
                dve.wait_ge(carry_ready, k + 1)
                dve.wait_ge(gmax_ready, k + 1)
                dve.tensor_tensor(delta, e_t, gmax[u][:, 0:CHUNK], ALU.subtract).then_inc(delta_ready, 1)
                dve.wait_ge(exps_ready, k + 1)
                d, dp = den[u], den[(u - 1) % ESLOTS]
                q, qp = num[u], num[(u - 1) % ESLOTS]
                dve.tensor_tensor(e_t, ex_t, zsT, ALU.mult).then_inc(w_ready, 1)
                dve.tensor_tensor_scan(d, c_t, ex_t, 0.0 if first else dp[:, CHUNK - 1:CHUNK], ALU.mult, ALU.add).then_inc(den_ready, 1)
                dve.wait_ge(w_ready, k + 1)
                dve.tensor_tensor_scan(q, c_t, e_t, 0.0 if first else qp[:, CHUNK - 1:CHUNK], ALU.mult, ALU.add).then_inc(num_ready, 1)
                dve.wait_ge(den_ready, k + 1)
                dve.wait_ge(num_ready, k + 1)
                if later(k, 1):
                    dve.wait_ge(L0["y_turned"], k)
                dve.reciprocal(y_t, d).then_inc(rec_ready, 1)
                dve.wait_ge(rec_ready, k + 1)
                dve.tensor_tensor(y_t, q, y_t, ALU.mult).then_inc(L0["y_ready"], 1)
            loop_steps(dve, EC, ESLOTS, step0)

            def stats(c, u):
                dve.wait_ge(node_turned, c + 1)
                pair = BANK_PAIR[u]
                dve.bn_stats(st0[:, bass.ds(2 * c, 1), :].rearrange("p o s -> p (o s)"), banks[pair][:, 0:3 * NPART])
                dve.bn_stats(st0[:, bass.ds(2 * c + 1, 1), :].rearrange("p o s -> p (o s)"), banks[pair + 1][:, 0:2 * NPART]).then_inc(stats0, 1)

            def scale_rows(c, u, i):
                dve.wait_ge(hout_loaded[u], loads_done(i))
                if later(c, NSLOTS):
                    dve.wait_ge(node_turned, c - NSLOTS + 1)
                    dve.wait_ge(kept, c - NSLOTS + 1)
                dve.tensor_tensor(nv[u], nx[u], snorm_sb[:, bass.ds(c * TPN, TPN)].unsqueeze(2).to_broadcast([NPART, TPN, D]), ALU.mult).then_inc(scaled, 1)
                if later(c, 1):
                    stats(c - 1, (u - 1) % NSLOTS)
            loop_steps(dve, NCH, NSLOTS, scale_rows)
            stats(NCH - 1, NSLOTS - 1)
            dve.wait_ge(stats0, NCH)
            dve.bn_aggr(mv0, st0[:, :, :].rearrange("p c s -> p (c s)")).then_inc(bn_step, 1)
            dve.wait_ge(bn_sqrt, 1)
            dve.reciprocal(rs_col, sd_col).then_inc(bn_step, 1)
            dve.wait_ge(bn_step, 2)
            dve.tensor_tensor(a_col, g0_col, rs_col, ALU.mult).then_inc(bn_step, 1)
            dve.wait_ge(bn_step, 3)
            dve.tensor_tensor(ma_col, mv0[:, 0:1], a_col, ALU.mult).then_inc(bn_step, 1)
            dve.wait_ge(bn_step, 4)
            dve.tensor_tensor(b_col, be0_col, ma_col, ALU.subtract).then_inc(bn_step, 1)
            dve.wait_ge(bn_step, 5)
            dve.tensor_copy(a_wide, a_col.to_broadcast([P, NPART])).then_inc(bn_step, 1)
            dve.wait_ge(kept, NCH)
            dve.wait_ge(node_turned, NCH)
            dve.tensor_copy(b_wide, b_col.to_broadcast([P, NPART])).then_inc(bn_step, 1)
            dve.wait_ge(ab_turned, 1)
            dve.tensor_copy(a_row[:, :], banks[4][0:NPART, 0:D]).then_inc(ab_ready, 1)
            dve.tensor_copy(b_row[:, :], banks[5][0:NPART, 0:D]).then_inc(ab_ready, 1)
            dve.wait_ge(ab_ready, 2)

            def finish_rows(c, u, i):
                rows = nodes[:, bass.ds(c * TPN, TPN), :]
                dve.wait_ge(elu_ready, c + 1)
                dve.wait_ge(x_loaded[u], loads_done(i))
                dve.scalar_tensor_tensor(out=nx[u], in0=ne[u], scalar=-1.0, in1=nx[u], op0=ALU.add, op1=ALU.add).then_inc(t_ready, 1)
                dve.wait_ge(t_ready, c + 1)
                dve.scalar_tensor_tensor(out=rows, in0=nv[u], scalar=0.0, in1=nx[u], op0=ALU.max, op1=ALU.add).then_inc(s_ready, 1)
                dve.wait_ge(s_ready, c + 1)
                for j in range(TPN):
                    last = dve.bn_stats(st1[:, bass.ds(c * TPN + j, 1), :].rearrange("p o s -> p (o s)"),
                                        nodes[:, bass.ds(c * TPN + j, 1), :].rearrange("p o f -> p (o f)"))
                last.then_inc(stats1, 1)

            def affine_rows(c, u, i):
                rows = nodes[:, bass.ds(c * TPN, TPN), :]
                dve.tensor_tensor(nv[u], rows, a_row[:, :].unsqueeze(1).to_broadcast([NPART, TPN, D]), ALU.mult).then_inc(va_ready, 1)
                dve.wait_ge(va_ready, c + 1)
                dve.tensor_tensor(nv[u], nv[u], b_row[:, :].unsqueeze(1).to_broadcast([NPART, TPN, D]), ALU.add).then_inc(v_ready, 1)
                if later(c, 1):
                    finish_rows(c - 1, (u - 1) % NSLOTS, i if u else i - 1)
            loop_steps(dve, NCH, NSLOTS, affine_rows)
            finish_rows(NCH - 1, NSLOTS - 1, NCH // NSLOTS - 1)
            dve.wait_ge(stats1, NCH)
            me, qe, mo, qo = (st1[:, :, i] for i in (1, 2, 4, 5))
            dve.tensor_tensor(m_s, me, mo, ALU.add).then_inc(ln_small, 1)
            dve.tensor_tensor(m_d, me, mo, ALU.subtract).then_inc(ln_small, 1)
            dve.tensor_tensor(v_s, qe, qo, ALU.add).then_inc(ln_small, 1)
            dve.wait_ge(ln_small, 3)
            dve.tensor_tensor(m_d, m_d, m_d, ALU.mult).then_inc(ln_step, 1)
            dve.tensor_scalar(v_s, v_s, 1.0 / D, None, ALU.mult).then_inc(ln_step, 1)
            dve.wait_ge(ln_step, 2)
            dve.scalar_tensor_tensor(out=v_q, in0=m_d, scalar=0.25, in1=v_s, op0=ALU.mult, op1=ALU.add).then_inc(ln_step, 1)
            dve.wait_ge(ln_sqrt, 1)
            dve.reciprocal(rstd1, v_s).then_inc(ln_step, 1)
            dve.wait_ge(ln_step, 4)
            dve.scalar_tensor_tensor(out=mb1, in0=m_s, scalar=-0.5, in1=rstd1, op0=ALU.mult, op1=ALU.mult).then_inc(ln_step, 1)
            dve.wait_ge(ln_step, 5)
            with dve.Fori(0, NCH) as c:
                for j in range(ACT_NORM_FROM):
                    row = nodes[:, bass.ds(c * TPN + j, 1), :].rearrange("p o f -> p (o f)")
                    a = dve.tensor_scalar(row, row, rstd1[:, bass.ds(c * TPN + j, 1)], mb1[:, bass.ds(c * TPN + j, 1)], ALU.mult, ALU.add)
                a.then_inc(norm_dve, 1)

            def step1(k, u, i):
                dve.wait_ge(L1["weight"], k + 1)
                if later(k, 1):
                    dve.wait_ge(L1["y_ready"], k)
                dve.tensor_tensor(msg, att_w, xsT, ALU.mult).then_inc(msg_ready, 1)
                dve.wait_ge(msg_ready, k + 1)
                dve.wait_ge(L1["gates"][u], loads_done(i))
                if later(k, ESLOTS):
                    dve.wait_ge(L1["y_turned"], k - ESLOTS + 1)
                dve.tensor_tensor_scan(aggT[u], gate_t[u][:, 0:CHUNK], msg,
                                       0.0 if not later(k, 1) else aggT[(u - 1) % ESLOTS][:, CHUNK - 1:CHUNK], ALU.mult, ALU.add).then_inc(L1["y_ready"], 1)
            loop_steps(dve, EC, ESLOTS, step1)

            def row_stats(c, u, src_rows, st_sem, mv_sem):
                for j in range(TPN):
                    last = dve.bn_stats(st2[:, u, j, :], src_rows[:, j, :])
                last.then_inc(st_sem, 1)
                dve.wait_ge(st_sem, c + 1)
                dve.nop(nofuse=True)
                for j in range(TPN):
                    last = dve.bn_aggr(mv2[:, u, j, :], st2[:, u, j, :])
                last.then_inc(mv_sem, 1)

            def norm_rows(c, u, i):
                rows = nodes[:, bass.ds(c * TPN, TPN), :]
                dve.wait_ge(agg_loaded[u], loads_done(i))
                dve.tensor_tensor(nx[u], nx[u], rows, ALU.add).then_inc(n2["att"], 1)
                dve.tensor_tensor(ne[u], rows, be1_row[:, :].unsqueeze(1).to_broadcast([NPART, TPN, D]), ALU.add).then_inc(n2["xb"], 1)
                dve.wait_ge(n2["att"], c + 1)
                row_stats(c, u, nx[u], n2["st"], n2["mv"])
                dve.wait_ge(n2["mv"], c + 1)
                for j in range(TPN):
                    last = dve.scalar_tensor_tensor(out=nv[u][:, j, :], in0=nx[u][:, j, :], scalar=mv2[:, u, j, 0:1], in1=g1_row[:, :], op0=ALU.subtract, op1=ALU.mult)
                last.then_inc(n2["t"], 1)
                dve.wait_ge(n2["sd"], c + 1)
                dve.reciprocal(rs2[:, u, :], rs2[:, u, :]).then_inc(n2["rs"], 1)
                dve.wait_ge(n2["rs"], c + 1)
                dve.wait_ge(n2["t"], c + 1)
                dve.wait_ge(n2["xb"], c + 1)
                for j in range(TPN):
                    last = dve.scalar_tensor_tensor(out=nv[u][:, j, :], in0=nv[u][:, j, :], scalar=rs2[:, u, j:j + 1], in1=ne[u][:, j, :], op0=ALU.mult, op1=ALU.add)
                last.then_inc(n2["s"], 1)
                dve.wait_ge(n2["s"], c + 1)
                row_stats(c, u, nv[u], n2["stb"], n2["mvb"])
                dve.wait_ge(n2["mvb"], c + 1)
                dve.wait_ge(n2["sdb"], c + 1)
                dve.reciprocal(rs2[:, u, :], rs2[:, u, :]).then_inc(n2["rsb"], 1)
                dve.wait_ge(n2["rsb"], c + 1)
                if later(c, NSLOTS):
                    dve.wait_ge(out_stored[u], 16 * i)
                for j in range(TPN):
                    last = dve.tensor_scalar(no[u][:, j, :], nv[u][:, j, :], mv2[:, u, j, 0:1], rs2[:, u, j:j + 1], ALU.subtract, ALU.mult)
                last.then_inc(n2["out"], 1)
            loop_steps(dve, NCH, NSLOTS, norm_rows)


_INS = ["x", "src", "dst", "node_vec1", "L0_gnn_W_fc", "L0_gnn_gamma", "L0_gnn_beta", "L1_gnn_W1", "L1_gnn_b1",
        "L1_gnn_W2", "L1_gnn_b2", "L1_gnn_gamma", "L1_gnn_beta"]


def kernel(**inputs):
    import numpy as _np
    import concourse.bacc as _bacc
    from concourse import mybir as _mybir
    from concourse.bass_utils import run_bass_kernel_spmd as _run

    nc = _bacc.Bacc("TRN2", target_bir_lowering=False, num_devices=1)
    arrays, args = {}, []
    for name in _INS:
        a = _np.ascontiguousarray(inputs[name])
        arrays[f"in_{name}"] = a
        args.append(nc.dram_tensor(f"in_{name}", a.shape, _mybir.dt.from_np(a.dtype), kind="ExternalInput").ap())
    out = nc.dram_tensor("out_0", inputs["x"].shape, _mybir.dt.float32, kind="ExternalOutput").ap()
    gnn_two_layers(nc, *args, out)
    r = _run(nc, [arrays], core_ids=[0])
    return r.results[0]["out_0"]
```

```python
from contextlib import ExitStack

import concourse.bass as bass
from concourse import mybir

F32 = mybir.dt.float32
BF16 = mybir.dt.bfloat16
I32 = mybir.dt.int32
FP16 = mybir.dt.float16
ALU = mybir.AluOpType
ACT = mybir.ActivationFunctionType

P = 128
EPS = 1e-5
N_CONSTS = 12
BN_STEPS = 7
X_PARTS = 5
BANK_PAIR = [0, 2, 4, 6, 2]
ACT_NORM_FROM = 3
LN_EXP_TABLES = 6
BIG = 1.6e38
PEELED = 3
ROWS = 125
TPC = 4
CHUNK = ROWS * TPC
ESLOTS = 3
BEHIND = 2 * ESLOTS
NPART = 120
TPN = 5
WINDOW = 4
WARM = 6
NSLOTS = 5


def later(k, n):
    return not isinstance(k, int) or k >= n


def pipeline(eng, count, slots, *stages):
    def step(k, u, i):
        for lag, fn in stages:
            if later(k, lag) and (not isinstance(k, int) or k - lag < count):
                fn(k - lag, (u - lag) % slots, i + (u - lag) // slots)
    for k in range(PEELED * slots):
        step(k, k % slots, k // slots)
    with eng.Fori(PEELED, count // slots) as i:
        for u in range(slots):
            step(i * slots + u, u, i)
    for k in range(count, count + max(lag for lag, _ in stages)):
        step(k, k % slots, k // slots)


def loads_done(i):
    return 16 * (i + 1)


def gnn_two_layers(nc, x, src, dst, snorm, w_fc, gamma0, beta0, w1, b1, w2, b2, gamma1, beta1, out):
    N, D = x.shape
    E = src.shape[0]
    assert N == E and D == P and E % (CHUNK * ESLOTS) == 0
    EC = E // CHUNK
    ET = E // ROWS
    PER_PART = N // NPART
    NCH = PER_PART // TPN
    EROWS = E // NPART
    HALVES = EROWS // ROWS
    assert PER_PART == HALVES * ROWS and WINDOW == TPC and TPC == ESLOTS + 1
    assert HALVES == 2 and NCH % NSLOTS == 0 and PER_PART * NPART == N

    keep_dram = nc.dram_tensor("keep_scratch", (E,), BF16, kind="Internal").ap()
    gate_dram = nc.dram_tensor("gate_scratch", (E,), BF16, kind="Internal").ap()
    hout_dram = nc.dram_tensor("hout_scratch", (N, D), F32, kind="Internal").ap()
    x1_dram = nc.dram_tensor("x1_scratch", (N, D), F32, kind="Internal").ap()
    agg_dram = nc.dram_tensor("agg_scratch", (N, D), F32, kind="Internal").ap()

    rel_dram = nc.dram_tensor("rel_scratch", (E,), FP16, kind="Internal").ap()
    first_dram = nc.dram_tensor("first_scratch", (ET,), I32, kind="Internal").ap()

    def node_chunk(table, c):
        return table[bass.ds(c * TPN * NPART, TPN * NPART), :].rearrange("(j p) f -> p j f", p=NPART)

    with ExitStack() as ctx:
        def sb(name, shape, dt=F32):
            return ctx.enter_context(nc.sbuf_tensor(name, shape, dt))

        def sem(name):
            return ctx.enter_context(nc.semaphore(name))

        def sems(name, n):
            return [sem(f"{name}{i}") for i in range(n)]

        psum = ctx.enter_context(nc.psum_tensor("psum", [P, 8 * 512], F32))
        banks = [psum[:, 512 * i:512 * (i + 1)] for i in range(8)]

        CW = TPN * D
        node_table = sb("node_table", [P, NCH * CW])

        def node_cols(c):
            return node_table[:, bass.ds(c * CW, TPN * NPART)]

        def node_rows(c):
            return node_table[0:NPART, bass.ds(c * CW, CW)].rearrange("p (j f) -> p j f", f=D)

        def node_row(c, j):
            return node_table[0:NPART, bass.ds(c * CW + j * D, D)]
        ARENA = 18270
        arena = sb("arena", [P, ARENA])

        def carve(sizes):
            at, views = 0, []
            for n in sizes:
                views.append(arena[:, at:at + n])
                at += n
            assert at <= ARENA, at
            return views

        SRC, DST, END = range(3)
        idx_all = sb("idx_all", [P, EC + BEHIND, 3, TPC], I32)
        idx_now = sb("idx_now", [P, ESLOTS, 3, TPC], I32)
        ident = sb("ident", [P, P])
        w_fc_sb = sb("w_fc_sb", [P, P])
        w_fcT = sb("w_fcT", [P, P])
        w1_sb = sb("w1_sb", [P, 2, P])
        w2_col = sb("w2_col", [P, 1])
        w2_wide = sb("w2_wide", [P, P])
        cols = sb("cols", [P, 16])
        b1_col, b2_col, g0_col, be0_col = (cols[:, i:i + 1] for i in range(4))
        eps_col, sd_col, rs_col, a_col, ma_col, b_col, na_col, nb_col = (cols[:, i:i + 1] for i in range(4, 12))
        mv0 = cols[:, 12:14]
        g1_row = sb("g1_row", [NPART, D])
        be1_row = sb("be1_row", [NPART, D])
        snorm_sb = sb("snorm_sb", [NPART, PER_PART])
        first_row = sb("first_row", [1, ET], I32)
        flag = sb("flag", [1, 1], I32)
        flag_f = sb("flag_f", [1, 1])
        win_i = sb("win_i", [NPART, WINDOW], I32)
        win_f = sb("win_f", [NPART, WINDOW])
        tcol = [sb(f"tcol{i}", [NPART, HALVES]) for i in range(7)]
        tcol_i = [sb(f"tcol_i{i}", [NPART, HALVES], I32) for i in range(2)]
        rel_max = sb("rel_max", [NPART, 1])

        A = carve([EROWS] * 12)
        snorm_in = A[10][0:ROWS, 0:HALVES * NPART].rearrange("p (h q) -> p h q", h=HALVES)
        rel_f = A[9][0:NPART]
        rel_h = A[11][0:NPART].bitcast(FP16)[:, 0:EROWS]
        src_i, dst_i, nxt_i, prv_i = (a[0:NPART].bitcast(I32) for a in A[0:4])
        src_f, dst_f, same_f, end_f = (a[0:NPART] for a in A[4:8])
        bf = A[8][0:NPART].bitcast(BF16)
        keep_b, gate_b = bf[:, 0:EROWS], bf[:, EROWS:2 * EROWS]
        ZER = max(TPN, TPC) * D
        HSLOTS = 3
        HALF_CHUNK = CHUNK // 2
        V = carve([TPC * D] * 9 + [CHUNK] * 11 + [CHUNK + 1] + [CHUNK // 2] * 2 * ESLOTS + [ZER] + [WINDOW * HALF_CHUNK] * HSLOTS + [WINDOW * D])
        rows_s = [v.rearrange("p (t f) -> p t f", f=D) for v in V[0:3]]
        rows_d = [v.rearrange("p (t f) -> p t f", f=D) for v in V[3:6]]
        rows_y = [v.rearrange("p (t f) -> p t f", f=D) for v in V[6:9]]
        xsT, xdT, zsT, e_t, delta, c_t, ex_t, den, num, y_t, rec_t = V[9:20]
        gmax = V[20]
        hid, att_w, msg = V[11:14]
        aggT = V[14:17]
        gate_t = [v.bitcast(BF16) for v in V[21:24]]
        rel_t = [v[0:NPART].bitcast(FP16) for v in V[24:27]]
        zeros = V[27]
        onehot = [v[0:NPART].rearrange("p (w e) -> p w e", w=WINDOW) for v in V[28:31]]
        window = [v[0:NPART] for v in V[3:6] + V[31:32]]
        NV = carve([TPN * D] * (4 * NSLOTS) + [PER_PART * 6] + [PER_PART] * 6 + [2 * NCH * 6] + [NSLOTS * TPN * 6] * 2
                   + [NSLOTS * TPN * 2] * 2 + [NSLOTS * TPN] * 4)
        relu_c, exp_c = ([v[:, 0:TPN * NPART] for v in NV[NSLOTS * i:NSLOTS * (i + 1)]] for i in (1, 2))
        nview = [v[0:NPART].rearrange("p (j f) -> p j f", f=D) for v in NV[0:4 * NSLOTS]]
        nx, nv, ne, no = (nview[NSLOTS * i:NSLOTS * (i + 1)] for i in range(4))
        st0 = NV[27].rearrange("p (c s) -> p c s", s=6)
        st1 = NV[20][0:NPART].rearrange("p (j s) -> p j s", s=6)
        m_s, m_d, v_s, v_q, rstd1, mb1 = (v[0:NPART] for v in NV[21:27])
        st2, st3 = (v[0:NPART].rearrange("p (u j s) -> p u j s", u=NSLOTS, s=6) for v in NV[28:30])
        mvA, mvB = (v[0:NPART].rearrange("p (u j s) -> p u j s", u=NSLOTS, s=2) for v in NV[30:32])
        rsA, mbA, rsB, mbB = (v[0:NPART].rearrange("p (u j) -> p u j", u=NSLOTS) for v in NV[32:36])
        carry = sb("carry", [P, 2])
        eps_n = sb("eps_n", [NPART, 1])

        consts = sem("consts")
        minus_one = sem("minus_one")
        shifted = sem("shifted")
        ident_zero = sem("ident_zero")
        ident_ready = sem("ident_ready")
        small = sem("small")
        tables = sem("tables")
        idx_turned = sem("idx_turned")
        idx_ready = sem("idx_ready")
        gates_stored = sem("gates_stored")
        zeros_ready = sem("zeros_ready")
        hout_zeroed = sem("hout_zeroed")
        agg_zeroed = sem("agg_zeroed")

        first_step = sem("first_step")
        rel_ready = sem("rel_ready")
        first_stored = sem("first_stored")
        first_ready = sem("first_ready")
        max_turned = sem("max_turned")
        flag_step = sem("flag_step")
        win_ready = sem("win_ready")
        snorm_ready = sem("snorm_ready")
        sums_carried = sem("sums_carried")
        x_resident = sem("x_resident")

        block = ctx.enter_context(nc.Block())

        def by_width(eng, edge_pass):
            is_narrow = eng.value_load(flag[0:1, 0:1], min_val=0, max_val=1)
            with eng.If(is_narrow == 1):
                edge_pass(True)
            with eng.Else():
                edge_pass(False)

        def gathers_dst(L, k, narrow):
            return not narrow or (L is L0 and isinstance(k, int) and k < WARM)

        def edge_sems(n):
            return dict(
                gathered=sems(f"gathered{n}_", ESLOTS), gates=sems(f"gates{n}_", ESLOTS),
                scattered=sems(f"scattered{n}_", ESLOTS), staged=sem(f"staged{n}"),
                turned=sem(f"turned{n}"), copied=sem(f"copied{n}"), product=sem(f"product{n}"),
                zs_copied=sem(f"zs_copied{n}"), weight=sem(f"weight{n}"), y_turned=sem(f"y_turned{n}"),
                y_rows=sem(f"y_rows{n}"), y_ready=sem(f"y_ready{n}"), logit=sem(f"logit{n}"),
                rel=sems(f"rel{n}_", ESLOTS), onehot=sem(f"onehot{n}"), window_copied=sem(f"window_copied{n}"), window_used=sem(f"window_used{n}"))
        L0, L1 = edge_sems(0), edge_sems(1)
        e_ready, carry_ready, gmax_ready, delta_ready = (sem(s) for s in ("e_ready", "carry_ready", "gmax_ready", "delta_ready"))
        act_step, exps_ready, w_ready, den_ready, num_ready = (sem(s) for s in ("act_step", "exps_ready", "w_ready", "den_ready", "num_ready"))
        rec_ready, ln_ready, ln_small = sem("rec_ready"), sem("ln_ready"), sem("ln_small")
        msg_ready = sem("msg_ready")
        hout_loaded = sems("hout_loaded", NSLOTS)
        kept = sem("kept")
        scaled, node_turned, stats0 = sem("scaled"), sem("node_turned"), sem("stats0")
        bn_step, bn_sqrt = sem("bn_step"), sem("bn_sqrt")
        x_loaded = sems("x_loaded", NSLOTS)
        neg_ready, pos_ready, exp_ready, elu_ready, elu_turned, s_ready = (
            sem(s) for s in ("neg_ready", "pos_ready", "exp_ready", "elu_ready", "elu_turned", "s_ready"))
        stats1, ln_step, ln_sqrt, norm_dve, norm_act = (sem(s) for s in ("stats1", "ln_step", "ln_sqrt", "norm_dve", "norm_act"))
        x1_stored = sem("x1_stored")
        agg_loaded = sems("agg_loaded", NSLOTS)
        out_stored = sems("out_stored", NSLOTS)
        n2 = {s: sem("n2_" + s) for s in ("att", "xb", "t", "s", "stA", "mvA", "sdA", "rsA", "mbA", "normA", "stB", "mvB", "sdB", "rsB", "mbB", "normB")}

        @block.sync
        def _(sp):
            col = lambda v: v.rearrange("(p o) -> p o", o=1)
            loads = [(src_i, src.rearrange("(p j) -> p j", p=NPART)),
                     (dst_i, dst.rearrange("(p j) -> p j", p=NPART)),
                     (w_fc_sb[:, :], w_fc), (w1_sb[:, :, :], w1.rearrange("(a k) h -> k a h", a=2)),
                     (w2_col[:, :], w2), (b1_col, col(b1)), (b2_col, b2.partition_broadcast(P)),
                     (g0_col, col(gamma0)), (be0_col, col(beta0)),
                     (g1_row[:, :], gamma1.partition_broadcast(NPART)),
                     (be1_row[:, :], beta1.partition_broadcast(NPART)),
                     (snorm_in[:, :, :], snorm.rearrange("(q h p) o -> q h (p o)", h=HALVES, p=NPART))]
            assert len(loads) == N_CONSTS
            for to, fr in loads:
                sp.dma_start(to, fr).then_inc(consts, 16)
            sp.wait_ge(minus_one, 1)
            last = (NPART - 1) * EROWS
            sp.dma_start(nxt_i[0:NPART - 1, :], dst[1:last + 1].rearrange("(p j) -> p j", j=EROWS)).then_inc(shifted, 16)
            sp.dma_start(nxt_i[NPART - 1:NPART, 0:EROWS - 1], dst[last + 1:E].rearrange("(p j) -> p j", p=1)).then_inc(shifted, 16)
            sp.dma_start(prv_i[0:1, 1:EROWS], dst[0:EROWS - 1].rearrange("(p j) -> p j", p=1)).then_inc(shifted, 16)
            sp.dma_start(prv_i[1:NPART, :], dst[EROWS - 1:E - 1].rearrange("(p j) -> p j", j=EROWS)).then_inc(shifted, 16)
            sp.wait_ge(tables, 6)
            sp.dma_start(keep_dram.rearrange("(p j) -> p j", p=NPART), keep_b).then_inc(gates_stored, 16)
            sp.dma_start(gate_dram.rearrange("(p j) -> p j", p=NPART), gate_b).then_inc(gates_stored, 16)
            sp.wait_ge(rel_ready, 3)
            sp.dma_start(rel_dram.rearrange("(p j) -> p j", p=NPART), rel_h).then_inc(gates_stored, 16)
            sp.dma_start(first_dram.rearrange("(q h) -> q h", h=HALVES), tcol_i[1][:, :]).then_inc(first_stored, 16)
            sp.wait_ge(first_stored, 16)
            sp.dma_start(first_row[:, :], first_dram.rearrange("(o t) -> o t", o=1)).then_inc(first_ready, 16)
            sp.wait_ge(gates_stored, 48)

            sp.wait_ge(zeros_ready, 1)
            def gate_load(L, table, used, zero, narrow):
                def step(k, u, i):
                    if narrow:
                        if later(k, ESLOTS):
                            sp.wait_ge(L["onehot"], 2 * (k - ESLOTS + 1))
                            sp.nop(nofuse=True)
                        sp.dma_start(rel_t[u], rel_dram[bass.ds(k * CHUNK, CHUNK)].partition_broadcast(NPART)).then_inc(L["rel"][u], 16)
                    if later(k, ESLOTS):
                        sp.wait_ge(used, k - ESLOTS + 1)
                        sp.nop(nofuse=True)
                    sp.dma_start(gate_t[u][:, 0:CHUNK], table[bass.ds(k * CHUNK, CHUNK)].partition_broadcast(P)).then_inc(L["gates"][u], 16)
                    if zero is not None:
                        sp.dma_start(zero[bass.ds(k * CHUNK, CHUNK), :].rearrange("(p t) f -> p t f", t=TPN),
                                     zeros[0:CHUNK // TPN, 0:CW].rearrange("p (t f) -> p t f", f=D)).then_inc(agg_zeroed, 16)
                return step
            sp.wait_ge(flag_step, 2)
            by_width(sp, lambda narrow: pipeline(sp, EC, ESLOTS, (0, gate_load(L0, gate_dram, gmax_ready, agg_dram, narrow))))

            for u in range(ESLOTS):
                sp.wait_ge(L0["scattered"][u], 16 * TPC * (EC // ESLOTS))
            def hout_load(c, u, i):
                if later(c, NSLOTS):
                    sp.wait_ge(scaled, c - NSLOTS + 1)
                sp.dma_start(nx[u], node_chunk(hout_dram, c)).then_inc(hout_loaded[u], 16)
            pipeline(sp, NCH, NSLOTS, (0, hout_load))
            def x_load(c, u, i):
                if later(c, NSLOTS):
                    sp.wait_ge(s_ready, c - NSLOTS + 1)
                sp.dma_start(nx[u], node_chunk(x, c)).then_inc(x_loaded[u], 16)
            sp.wait_ge(scaled, NCH)
            pipeline(sp, NCH, NSLOTS, (0, x_load))
            with sp.Fori(0, NCH) as c:
                sp.wait_ge(norm_dve, c + 1)
                sp.wait_ge(norm_act, c + 1)
                sp.dma_start(node_chunk(x1_dram, c), node_rows(c)).then_inc(x1_stored, 16)

            by_width(sp, lambda narrow: pipeline(sp, EC, ESLOTS, (0, gate_load(L1, keep_dram, L1["y_ready"], None, narrow))))

            for u in range(ESLOTS):
                sp.wait_ge(L1["scattered"][u], 16 * TPC * (EC // ESLOTS))
            def agg_load(c, u, i):
                if later(c, NSLOTS):
                    sp.wait_ge(n2["normA"], c - NSLOTS + 1)
                sp.dma_start(nx[u], node_chunk(agg_dram, c)).then_inc(agg_loaded[u], 16)
            def out_store(c, u, i):
                sp.wait_ge(n2["normB"], c + 1)
                sp.dma_start(node_chunk(out, c), no[u]).then_inc(out_stored[u], 16)
            pipeline(sp, NCH, NSLOTS, (0, agg_load), (4, out_store))
            for u in range(NSLOTS):
                sp.wait_ge(out_stored[u], 16 * (NCH // NSLOTS))

        @block.gpsimd
        def _(pool):
            pool.memset(nxt_i, -1)
            pool.memset(prv_i, -1).then_inc(minus_one, 1)
            pool.memset(zeros, 0.0).then_inc(zeros_ready, 1)
            pool.memset(ident[:, :], 0.0).then_inc(ident_zero, 1)
            pool.wait_ge(ident_zero, 1)
            pool.affine_select(out=ident[:, :], in_=ident[:, :], compare_op=ALU.not_equal, fill=1.0, base=0,
                               pattern=[[-1, P]], channel_multiplier=1).then_inc(ident_ready, 1)

            pool.iota(win_i[:, :], pattern=[[NPART, WINDOW]], base=0, channel_multiplier=1).then_inc(win_ready, 1)

            def gather(L, table, k, u, i, narrow):
                if later(k, ESLOTS):
                    pool.wait_ge(L["turned"], k - ESLOTS + 1)
                    pool.nop(nofuse=True)
                if later(k, BEHIND + ESLOTS):
                    pool.wait_ge(L["scattered"][u], (i - BEHIND // ESLOTS) * 16 * TPC)
                pool.tensor_copy(idx_now[0:ROWS, u, :, :],
                                 idx_all[0:ROWS, bass.ds(k, 1), :, :].rearrange("r o n t -> r (o n) t")).then_inc(L["staged"], 1)
                pool.wait_ge(L["staged"], k + 1)
                pool.nop(nofuse=True)
                ends = [(SRC, rows_s)] + [(DST, rows_d)] * gathers_dst(L, k, narrow)
                for t in range(TPC):
                    for n, rows in ends:
                        pool.indirect_dma_start(
                            out=rows[u][0:ROWS, t, :], out_offset=None, in_=table,
                            in_offset=bass.IndirectOffsetOnAxis(ap=idx_now[0:ROWS, u, n, t:t + 1], axis=0),
                        ).then_inc(L["gathered"][u], 16)

            def scatter(L, table, k, u):
                pool.wait_ge(L["y_rows"], k + 1)
                pool.nop(nofuse=True)
                for t in range(TPC):
                    pool.indirect_dma_start(
                        out=table, out_offset=bass.IndirectOffsetOnAxis(ap=idx_now[0:ROWS, u, END, t:t + 1], axis=0),
                        in_=rows_y[u][0:ROWS, t, :], in_offset=None, bounds_check=N - 1, oob_is_err=False,
                    ).then_inc(L["scattered"][u], 16)

            def edge_pass(L, table, result, zeroed, chunks, narrow):
                for k in range(PEELED * ESLOTS):
                    gather(L, table, k, k % ESLOTS, k // ESLOTS, narrow)
                    if k == BEHIND:
                        pool.wait_ge(zeroed, 16 * chunks)
                    if k >= BEHIND:
                        scatter(L, result, k - BEHIND, k % ESLOTS)
                with pool.Fori(PEELED, EC // ESLOTS) as i:
                    for u in range(ESLOTS):
                        gather(L, table, i * ESLOTS + u, u, i, narrow)
                        scatter(L, result, i * ESLOTS + u - BEHIND, u)
                for k in range(EC, EC + BEHIND):
                    u = k % ESLOTS
                    pool.wait_ge(L["scattered"][u], (k // ESLOTS - BEHIND // ESLOTS) * 16 * TPC)
                    pool.tensor_copy(idx_now[0:ROWS, u, END, :], idx_all[0:ROWS, k, END, :]).then_inc(L["staged"], 1)
                    pool.wait_ge(L["staged"], k + 1)
                    scatter(L, result, k - BEHIND, u)

            pool.wait_ge(idx_ready, 3)
            pool.wait_ge(gates_stored, 48)
            pool.wait_ge(max_turned, 2)
            pool.wait_ge(flag_step, 2)
            by_width(pool, lambda narrow: edge_pass(L0, x, hout_dram, hout_zeroed, NCH, narrow))
            pool.wait_ge(x1_stored, 16 * NCH)
            by_width(pool, lambda narrow: edge_pass(L1, x1_dram, agg_dram, agg_zeroed, EC, narrow))

            def add_rows(c, u, i):
                pool.wait_ge(agg_loaded[u], loads_done(i))
                pool.nop(nofuse=True)
                pool.tensor_tensor(nx[u], nx[u], node_rows(c), ALU.add).then_inc(n2["att"], 1)
                if later(c, NSLOTS):
                    pool.wait_ge(n2["mvB"], c - NSLOTS + 1)
                    pool.nop(nofuse=True)
                pool.tensor_tensor(ne[u], node_rows(c), be1_row[:, :].unsqueeze(1).to_broadcast([NPART, TPN, D]), ALU.add).then_inc(n2["xb"], 1)
            pipeline(pool, NCH, NSLOTS, (0, add_rows))

        @block.tensor
        def _(pe):
            pe.wait_ge(ident_ready, 1)
            pe.wait_ge(consts, 16 * N_CONSTS)
            pe.wait_ge(tables, 3)
            for n, tab in enumerate((src_f, dst_f, end_f)):
                for h in range(HALVES):
                    mm = pe.transpose(banks[n][0:ROWS, h * NPART:(h + 1) * NPART],
                                      tab[:, h * ROWS:(h + 1) * ROWS], ident[0:NPART, 0:NPART])
                mm.then_inc(idx_turned, 1)
            pe.transpose(banks[3][:, 0:P], w_fc_sb[:, :], ident[:, :]).then_inc(idx_turned, 1)

            pe.wait_ge(rel_ready, 4)
            pe.transpose(banks[4][0:1, 0:NPART], rel_max[:, :], ident[0:NPART, 0:NPART]).then_inc(max_turned, 1)
            for h in range(HALVES):
                mm = pe.transpose(banks[5][0:NPART, h * ROWS:(h + 1) * ROWS], snorm_in[:, h, :], ident[0:ROWS, 0:ROWS])
            mm.then_inc(max_turned, 1)

            def expand(L, narrow):
                def stage(k, u, i):
                    if not narrow:
                        return
                    if gathers_dst(L, k, narrow):
                        pe.nop(nofuse=True).then_inc(L["window_used"], TPC)
                        return
                    if later(k, ESLOTS):
                        pe.wait_ge(L["copied"], k - ESLOTS + 1)
                    for t in range(TPC):
                        half, e = divmod(t * ROWS, HALF_CHUNK)
                        if e == 0:
                            pe.wait_ge(L["onehot"], 2 * k + half + 1)
                        pe.wait_ge(L["window_copied"], k * TPC + t + 1)
                        for w in range(WINDOW):
                            mm = pe.matmul(banks[5 + u][:, t * ROWS:(t + 1) * ROWS], window[t][:, w * D:(w + 1) * D],
                                           onehot[(2 * u + half) % HSLOTS][:, w, e:e + ROWS], start=(w == 0), stop=(w == WINDOW - 1))
                        mm.then_inc(L["window_used"], 1)
                return stage

            def turn(L, narrow):
                def stage(k, u, i):
                    both = gathers_dst(L, k, narrow)
                    if both:
                        pe.wait_ge(L["gathered"][u], (i + 1) * 32 * TPC)
                    else:
                        warm = len(range(u, WARM, ESLOTS)) if L is L0 else 0
                        pe.wait_ge(L["gathered"][u], (i + 1 + warm) * 16 * TPC)
                    if later(k, 1):
                        pe.wait_ge(L["copied"], k)
                    for bank, rows in ((0, rows_s), (1, rows_d))[:1 + both]:
                        for t in range(TPC):
                            mm = pe.transpose(banks[bank][:, t * ROWS:(t + 1) * ROWS], rows[u][0:ROWS, t, :], ident[0:ROWS, 0:ROWS])
                    mm.then_inc(L["turned"], 1)
                return stage

            def turn_back(L, ys):
                def stage(k, u, i):
                    pe.wait_ge(L["y_ready"], k + 1)
                    if later(k, 1):
                        pe.wait_ge(L["y_rows"], k)
                    for t in range(TPC):
                        mm = pe.transpose(banks[4][0:ROWS, t * D:(t + 1) * D], ys[u][:, t * ROWS:(t + 1) * ROWS], ident[:, :])
                    mm.then_inc(L["y_turned"], 1)
                return stage

            def products0(k, u, i):
                pe.wait_ge(L0["copied"], k + 1)
                if later(k, 1):
                    pe.wait_ge(L0["zs_copied"], k)
                    pe.wait_ge(e_ready, k)
                pe.matmul(banks[2][:, 0:CHUNK], w_fcT[:, :], xsT, start=True, stop=True)
                pe.matmul(banks[3][:, 0:CHUNK], w_fcT[:, :], xdT, start=True, stop=True).then_inc(L0["product"], 1)
            pe.wait_ge(idx_ready, 4)
            pe.wait_ge(flag_step, 2)
            pe.wait_ge(first_ready, 16)
            by_width(pe, lambda narrow: pipeline(pe, EC, ESLOTS, (2, products0), (4, turn_back(L0, [y_t] * ESLOTS)),
                                                 (1, turn(L0, narrow)), (1, expand(L0, narrow))))

            def turn_nodes(c, u, i):
                pe.wait_ge(scaled, c + 1)
                if later(c, 2):
                    pe.wait_ge(kept, c - 1)
                pair = BANK_PAIR[u]
                for j in range(TPN):
                    mm = pe.transpose(banks[pair + j // 3][:, (j % 3) * NPART:(j % 3 + 1) * NPART],
                                      nv[u][:, j, :], ident[0:NPART, 0:NPART])
                mm.then_inc(node_turned, 1)
            pe.wait_ge(L0["y_rows"], EC)
            pipeline(pe, NCH, NSLOTS, (0, turn_nodes))
            def turn_elu(c, u, i):
                pe.wait_ge(elu_ready, c + 1)
                if later(c, 2):
                    pe.wait_ge(s_ready, c - 1)
                pair = BANK_PAIR[u]
                for j in range(TPN):
                    mm = pe.transpose(psum[0:NPART, pair * 512 + j * D:pair * 512 + (j + 1) * D],
                                      relu_c[u][:, j * NPART:(j + 1) * NPART], ident[:, :])
                mm.then_inc(elu_turned, 1)
            pipeline(pe, NCH, NSLOTS, (0, turn_elu))

            def hidden1(k, u, i):
                pe.wait_ge(L1["copied"], k + 1)
                if later(k, 1):
                    pe.wait_ge(L1["zs_copied"], k)
                pe.matmul(banks[2][:, 0:CHUNK], w1_sb[:, 0, :], xsT, start=True, stop=False)
                pe.matmul(banks[2][:, 0:CHUNK], w1_sb[:, 1, :], xdT, start=False, stop=True).then_inc(L1["product"], 1)
            def logit1(k, u, i):
                pe.wait_ge(L1["zs_copied"], k + 1)
                if later(k, 1):
                    pe.wait_ge(L1["weight"], k)
                pe.matmul(banks[3][:, 0:CHUNK], w2_wide[:, :], hid, start=True, stop=True).then_inc(L1["logit"], 1)
            pe.wait_ge(s_ready, NCH)
            by_width(pe, lambda narrow: pipeline(pe, EC, ESLOTS, (2, hidden1), (3, turn_back(L1, aggT)), (1, turn(L1, narrow)),
                                                 (2, logit1), (1, expand(L1, narrow))))

        @block.scalar
        def _(act):
            act.wait_ge(zeros_ready, 1)
            with act.Fori(0, NCH) as c:
                act.dma_start(node_chunk(hout_dram, c), zeros[0:NPART, 0:CW].rearrange("p (j f) -> p j f", f=D)).then_inc(hout_zeroed, 16)

            for c in range(X_PARTS):
                w = PER_PART // X_PARTS
                act.dma_start(node_table[0:NPART, c * w * D:(c + 1) * w * D].rearrange("p (t f) -> p t f", f=D),
                             x[c * w * NPART:(c + 1) * w * NPART, :].rearrange("(t p) f -> p t f", p=NPART)).then_inc(x_resident, 16)

            def copy_windows(L, narrow):
                def stage(k, u, i):
                    if not narrow:
                        return
                    if gathers_dst(L, k, narrow):
                        if k == WARM - 1:
                            act.wait_ge(x_resident, 16 * X_PARTS)
                        act.nop(nofuse=True).then_inc(L["window_copied"], TPC)
                        return
                    if L is L0 and isinstance(k, int) and k == WARM:
                        act.wait_ge(L["turned"], WARM)
                    _, firsts = nc.values_load_multi_w_load_instructions(
                        first_row[0:1, bass.ds(k * TPC, TPC)], engines=(mybir.EngineType.Activation,), min_val=0, max_val=PER_PART - WINDOW,
                        skip_runtime_bounds_check_because="VectorE bounds it")
                    for t, first in enumerate(firsts):
                        if later(k, 1):
                            act.wait_ge(L["window_used"], (k - 1) * TPC + t + 1)
                            act.nop(nofuse=True)
                        act.copy(window[t], node_table[0:NPART, bass.ds(first * D, WINDOW * D)]).then_inc(L["window_copied"], 1)
                return stage

            def copy_in(L, free, narrow):
                def stage(k, u, i):
                    act.wait_ge(L["turned"], k + 1)
                    if later(k, 1):
                        act.wait_ge(free, k)
                    act.copy(xsT, banks[0][:, 0:CHUNK])
                    if not gathers_dst(L, k, narrow):
                        act.wait_ge(L["window_used"], (k + 1) * TPC)
                    act.copy(xdT, banks[1 if gathers_dst(L, k, narrow) else 5 + u][:, 0:CHUNK]).then_inc(L["copied"], 1)
                return stage

            def copy_rows(L):
                def stage(k, u, i):
                    act.wait_ge(L["y_turned"], k + 1)
                    if later(k, ESLOTS):
                        act.wait_ge(L["scattered"][u], i * 16 * TPC)
                    act.copy(rows_y[u][0:ROWS], banks[4][0:ROWS, :].rearrange("p (t f) -> p t f", f=D)).then_inc(L["y_rows"], 1)
                return stage

            def copy_zs(k, u, i):
                act.wait_ge(L0["product"], k + 1)
                if later(k, 1):
                    act.wait_ge(w_ready, k)
                act.copy(zsT, banks[2][:, 0:CHUNK]).then_inc(L0["zs_copied"], 1)

            def reciprocal0(k, u, i):
                act.wait_ge(den_ready, k + 1)
                if later(k, 1):
                    act.wait_ge(L0["y_ready"], k)
                act.activation(rec_t, den, ACT.Ln).then_inc(ln_ready, 1)
                act.wait_ge(ln_ready, k + 1)
                act.activation(rec_t, rec_t, ACT.Exp, scale=-1.0).then_inc(rec_ready, 1)

            def exps0(k, u, i):
                act.wait_ge(delta_ready, k + 1)
                if later(k, 1):
                    act.wait_ge(num_ready, k)
                act.activation(c_t, delta, ACT.Relu).then_inc(act_step, 1)
                act.activation(ex_t, delta, ACT.Relu, scale=-1.0).then_inc(act_step, 1)
                act.wait_ge(act_step, 2 * k + 2)
                act.activation(c_t, c_t, ACT.Exp, scale=-1.0)
                act.activation(ex_t, ex_t, ACT.Exp, scale=-1.0).then_inc(exps_ready, 1)
            act.wait_ge(flag_step, 2)
            act.wait_ge(first_ready, 16)
            act.add_instruction(mybir.InstLoadActFuncSet(name=nc.get_next_instruction_name(), act_func_set_id=LN_EXP_TABLES, engine=mybir.EngineType.Activation))
            by_width(act, lambda narrow: pipeline(act, EC, ESLOTS, (2, copy_zs), (3, reciprocal0), (1, copy_windows(L0, narrow)), (4, copy_rows(L0)),
                                                  (2, exps0), (1, copy_in(L0, L0["product"], narrow))))
            act.wait_ge(x_resident, 16 * X_PARTS)

            def keep_cols(c, u, i):
                act.wait_ge(node_turned, c + 1)
                pair = BANK_PAIR[u]
                act.copy(node_table[:, bass.ds(c * CW, 3 * NPART)], banks[pair][:, 0:3 * NPART])
                act.copy(node_table[:, bass.ds(c * CW + 3 * NPART, 2 * NPART)], banks[pair + 1][:, 0:2 * NPART]).then_inc(kept, 1)
            pipeline(act, NCH, NSLOTS, (0, keep_cols))
            act.wait_ge(bn_step, 1)
            act.activation(sd_col, mv0[:, 1:2], ACT.Sqrt, bias=eps_col).then_inc(bn_sqrt, 1)
            act.wait_ge(bn_step, BN_STEPS)
            def elu(c, u, i):
                if later(c, NSLOTS):
                    act.wait_ge(elu_turned, c - NSLOTS + 1)
                act.activation(exp_c[u], node_cols(c), ACT.Relu, scale=na_col, bias=nb_col).then_inc(neg_ready, 1)
                act.activation(relu_c[u], node_cols(c), ACT.Relu, scale=a_col, bias=b_col).then_inc(pos_ready, 1)
                act.wait_ge(neg_ready, c + 1)
                act.activation(exp_c[u], exp_c[u], ACT.Exp, scale=-1.0).then_inc(exp_ready, 1)
            pipeline(act, NCH, NSLOTS, (0, elu))
            act.wait_ge(ln_step, 3)
            act.activation(v_s, v_q, ACT.Sqrt, bias=eps_n[:, :]).then_inc(ln_sqrt, 1)
            act.wait_ge(ln_step, 5)
            with act.Fori(0, NCH) as c:
                for j in range(ACT_NORM_FROM, TPN):
                    row = node_row(c, j)
                    a = act.activation(row, row, ACT.Identity, bias=mb1[:, bass.ds(c * TPN + j, 1)], scale=rstd1[:, bass.ds(c * TPN + j, 1)])
                a.then_inc(norm_act, 1)

            def relu1(k, u, i):
                act.wait_ge(L1["product"], k + 1)
                if later(k, 1):
                    act.wait_ge(L1["logit"], k)
                act.activation(hid, banks[2][:, 0:CHUNK], ACT.Relu, bias=b1_col).then_inc(L1["zs_copied"], 1)
            def sigmoid1(k, u, i):
                act.wait_ge(L1["logit"], k + 1)
                if later(k, 1):
                    act.wait_ge(msg_ready, k)
                act.activation(att_w, banks[3][:, 0:CHUNK], ACT.Sigmoid, bias=b2_col).then_inc(L1["weight"], 1)
            act.wait_ge(x1_stored, 16 * NCH)
            by_width(act, lambda narrow: pipeline(act, EC, ESLOTS, (2, relu1), (1, copy_windows(L1, narrow)), (3, copy_rows(L1)),
                                                  (2, sigmoid1), (1, copy_in(L1, msg_ready, narrow))))

            def root(mv, rs, ready, done):
                def stage(c, u, i):
                    act.wait_ge(ready, c + 1)
                    act.activation(rs[:, u, :], mv[:, u, :, 1:2].rearrange("p j o -> p (j o)"), ACT.Sqrt, bias=eps_n[:, :]).then_inc(done, 1)
                return stage
            def norm_a(c, u, i):
                act.wait_ge(n2["mbA"], c + 1)
                if later(c, NSLOTS):
                    act.wait_ge(n2["normB"], c - NSLOTS + 1)
                for j in range(TPN):
                    last = act.activation(nv[u][:, j, :], nx[u][:, j, :], ACT.Identity, bias=mbA[:, u, j:j + 1], scale=rsA[:, u, j:j + 1])
                last.then_inc(n2["normA"], 1)
            def norm_b(c, u, i):
                act.wait_ge(n2["mbB"], c + 1)
                if later(c, NSLOTS):
                    act.wait_ge(out_stored[u], 16 * i)
                for j in range(TPN):
                    last = act.activation(no[u][:, j, :], nv[u][:, j, :], ACT.Identity, bias=mbB[:, u, j:j + 1], scale=rsB[:, u, j:j + 1])
                last.then_inc(n2["normB"], 1)
            pipeline(act, NCH, NSLOTS, (0, root(mvA, rsA, n2["mvA"], n2["sdA"])), (1, norm_a),
                     (2, root(mvB, rsB, n2["mvB"], n2["sdB"])), (3, norm_b))

        @block.vector
        def _(dve):
            dve.memset(idx_all[:, 0:BEHIND, END, :], 0)
            dve.memset(eps_col, EPS)
            dve.memset(eps_n[:, :], EPS)
            dve.wait_ge(consts, 16 * N_CONSTS)
            dve.wait_ge(shifted, 64)
            dve.tensor_copy(src_f, src_i).then_inc(tables, 1)
            dve.tensor_copy(dst_f, dst_i).then_inc(tables, 1)
            dve.tensor_tensor(same_f, dst_i, nxt_i, ALU.is_equal).then_inc(small, 1)
            dve.wait_ge(small, 1)
            dve.wait_ge(tables, 2)
            dve.scalar_tensor_tensor(out=end_f, in0=same_f, scalar=float(N), in1=dst_f, op0=ALU.mult, op1=ALU.add).then_inc(tables, 1)
            dve.tensor_tensor(keep_b, dst_i, prv_i, ALU.is_equal).then_inc(tables, 1)
            dve.tensor_scalar(gate_b, same_f, 2 * BIG, -BIG, ALU.mult, ALU.add).then_inc(tables, 1)
            dve.tensor_copy(w2_wide[:, :], w2_col[:, 0:1].to_broadcast([P, P])).then_inc(tables, 1)
            for n, first in ((SRC, 0), (DST, 0), (END, BEHIND)):
                dve.wait_ge(idx_turned, n + 1)
                for h in range(HALVES):
                    last = dve.tensor_copy(idx_all[0:ROWS, first:first + EC, n, h::HALVES],
                                           banks[n][0:ROWS, h * NPART:(h + 1) * NPART].rearrange("r (k t) -> r k t", k=EC))
                last.then_inc(idx_ready, 1)
            dve.wait_ge(idx_turned, 4)
            dve.tensor_copy(w_fcT[:, :], banks[3][:, 0:P]).then_inc(idx_ready, 1)
            d0 = dst_f[:, 0:EROWS:ROWS]
            quot, quot_f, rest, low, high, first_f, first_node = (t[:, :] for t in tcol)
            def link(ins, n):
                ins.then_inc(first_step, 1)
                dve.wait_ge(first_step, n)
            link(dve.tensor_scalar(quot, d0, 1.0 / NPART, 0.5 / NPART - 0.5, ALU.mult, ALU.add), 1)
            link(dve.tensor_copy(tcol_i[0][:, :], quot), 2)
            link(dve.tensor_copy(quot_f, tcol_i[0][:, :]), 3)
            link(dve.scalar_tensor_tensor(out=rest, in0=quot_f, scalar=-float(NPART), in1=d0, op0=ALU.mult, op1=ALU.add), 4)
            link(dve.tensor_scalar(low, rest, 0.0, None, ALU.is_lt), 5)
            link(dve.tensor_scalar(high, rest, float(NPART), None, ALU.is_ge), 6)
            link(dve.tensor_tensor(first_f, quot_f, low, ALU.subtract), 7)
            link(dve.tensor_tensor(first_f, first_f, high, ALU.add), 8)
            link(dve.tensor_scalar(first_f, first_f, float(PER_PART - WINDOW), None, ALU.min), 9)
            dve.tensor_copy(tcol_i[1][:, :], first_f).then_inc(rel_ready, 1)
            link(dve.tensor_scalar(first_node, first_f, float(NPART), None, ALU.mult), 10)
            dve.tensor_tensor(rel_f.rearrange("p (h r) -> p h r", h=HALVES), dst_f.rearrange("p (h r) -> p h r", h=HALVES),
                              first_node.unsqueeze(2).to_broadcast([NPART, HALVES, ROWS]), ALU.subtract).then_inc(rel_ready, 1)
            dve.wait_ge(rel_ready, 2)
            dve.tensor_copy(rel_h, rel_f).then_inc(rel_ready, 1)
            dve.tensor_reduce(rel_max[:, :], rel_f, mybir.AxisListType.X, ALU.max).then_inc(rel_ready, 1)
            dve.wait_ge(win_ready, 1)
            dve.tensor_copy(win_f[:, :], win_i[:, :]).then_inc(rel_ready, 1)
            dve.wait_ge(max_turned, 1)
            dve.tensor_reduce(flag_f[:, :], banks[4][0:1, 0:NPART], mybir.AxisListType.X, ALU.max).then_inc(flag_step, 1)
            dve.wait_ge(flag_step, 1)
            dve.tensor_scalar(flag[:, :], flag_f[:, :], float(WINDOW * NPART), None, ALU.is_lt).then_inc(flag_step, 1)
            dve.wait_ge(max_turned, 2)
            dve.tensor_copy(snorm_sb[:, :].rearrange("p (q h) -> p h q", h=HALVES),
                            banks[5][0:NPART, 0:PER_PART].rearrange("p (h q) -> p h q", h=HALVES)).then_inc(snorm_ready, 1)
            dve.wait_ge(rel_ready, 5)
            dve.wait_ge(snorm_ready, 1)
            dve.wait_ge(flag_step, 2)
            dve.wait_ge(gates_stored, 48)
            dve.wait_ge(idx_ready, 4)
            dve.memset(gmax[:, 0:1], -BIG).then_inc(carry_ready, 1)
            dve.memset(carry[:, :], 0.0).then_inc(sums_carried, 1)

            def make_onehot(L, narrow):
                def stage(k, u, i):
                    if not narrow:
                        return
                    dve.wait_ge(L["rel"][u], loads_done(i))
                    if gathers_dst(L, k, narrow):
                        dve.nop(nofuse=True).then_inc(L["onehot"], 2)
                        return
                    for half in range(2):
                        if later(k, 2 - half):
                            dve.wait_ge(L["window_used"], (2 * k + half - HSLOTS + 1) * (TPC // 2))
                        dve.tensor_tensor(onehot[(2 * u + half) % HSLOTS],
                                          rel_t[u][:, half * HALF_CHUNK:(half + 1) * HALF_CHUNK].unsqueeze(1).to_broadcast([NPART, WINDOW, HALF_CHUNK]),
                                          win_f[:, :].unsqueeze(2).to_broadcast([NPART, WINDOW, HALF_CHUNK]), ALU.is_equal).then_inc(L["onehot"], 1)
                return stage

            def running_max0(k, u, i):
                dve.wait_ge(L0["zs_copied"], k + 1)
                if later(k, 1):
                    dve.wait_ge(num_ready, k)
                dve.tensor_tensor(e_t, banks[3][:, 0:CHUNK], zsT, ALU.mult).then_inc(e_ready, 1)
                if later(k, 1):
                    dve.wait_ge(gmax_ready, k)
                    dve.tensor_copy(gmax[:, 0:1], gmax[:, CHUNK:CHUNK + 1]).then_inc(carry_ready, 1)
                dve.wait_ge(e_ready, k + 1)
                dve.wait_ge(carry_ready, k + 1)
                dve.wait_ge(L0["gates"][u], loads_done(i))
                dve.tensor_tensor_scan(gmax[:, 1:CHUNK + 1], e_t, gate_t[u][:, 0:CHUNK], gmax[:, 0:1], ALU.max, ALU.min).then_inc(gmax_ready, 1)
                dve.wait_ge(gmax_ready, k + 1)
                dve.tensor_tensor(delta, e_t, gmax[:, 0:CHUNK], ALU.subtract).then_inc(delta_ready, 1)

            def sums0(k, u, i):
                dve.wait_ge(exps_ready, k + 1)
                dve.tensor_tensor(e_t, ex_t, zsT, ALU.mult).then_inc(w_ready, 1)
                if later(k, 1):
                    dve.wait_ge(num_ready, k)
                    dve.tensor_copy(carry[:, 0:1], den[:, CHUNK - 1:CHUNK])
                    dve.tensor_copy(carry[:, 1:2], num[:, CHUNK - 1:CHUNK]).then_inc(sums_carried, 1)
                    dve.wait_ge(L0["y_ready"], k)
                dve.wait_ge(sums_carried, k + 1)
                dve.tensor_tensor_scan(den, c_t, ex_t, carry[:, 0:1], ALU.mult, ALU.add).then_inc(den_ready, 1)
                dve.wait_ge(w_ready, k + 1)
                dve.tensor_tensor_scan(num, c_t, e_t, carry[:, 1:2], ALU.mult, ALU.add).then_inc(num_ready, 1)

            def divide0(k, u, i):
                dve.wait_ge(rec_ready, k + 1)
                if later(k, 1):
                    dve.wait_ge(L0["y_turned"], k)
                dve.wait_ge(num_ready, k + 1)
                dve.tensor_tensor(y_t, num, rec_t, ALU.mult).then_inc(L0["y_ready"], 1)
            by_width(dve, lambda narrow: pipeline(dve, EC, ESLOTS, (2, running_max0), (0, make_onehot(L0, narrow)), (3, divide0), (2, sums0)))

            HALF = TPN * NPART // 2
            def stats(c, u, i):
                dve.wait_ge(kept, c + 1)
                for h in range(2):
                    last = dve.bn_stats(st0[:, bass.ds(2 * c + h, 1), :].rearrange("p o s -> p (o s)"),
                                        node_table[:, bass.ds(c * CW + h * HALF, HALF)])
                last.then_inc(stats0, 1)

            def scale_rows(c, u, i):
                dve.wait_ge(hout_loaded[u], loads_done(i))
                if later(c, NSLOTS):
                    dve.wait_ge(node_turned, c - NSLOTS + 1)
                dve.tensor_tensor(nv[u], nx[u], snorm_sb[:, bass.ds(c * TPN, TPN)].unsqueeze(2).to_broadcast([NPART, TPN, D]), ALU.mult).then_inc(scaled, 1)
            pipeline(dve, NCH, NSLOTS, (0, scale_rows), (2, stats))
            dve.wait_ge(stats0, NCH)
            dve.bn_aggr(mv0, st0[:, :, :].rearrange("p c s -> p (c s)")).then_inc(bn_step, 1)
            dve.wait_ge(bn_sqrt, 1)
            dve.reciprocal(rs_col, sd_col).then_inc(bn_step, 1)
            dve.wait_ge(bn_step, 2)
            dve.tensor_tensor(a_col, g0_col, rs_col, ALU.mult).then_inc(bn_step, 1)
            dve.wait_ge(bn_step, 3)
            dve.tensor_tensor(ma_col, mv0[:, 0:1], a_col, ALU.mult).then_inc(bn_step, 1)
            dve.wait_ge(bn_step, 4)
            dve.tensor_tensor(b_col, be0_col, ma_col, ALU.subtract).then_inc(bn_step, 1)
            dve.wait_ge(bn_step, 5)
            dve.tensor_scalar(na_col, a_col, -1.0, None, ALU.mult).then_inc(bn_step, 1)
            dve.tensor_scalar(nb_col, b_col, -1.0, None, ALU.mult).then_inc(bn_step, 1)
            dve.wait_ge(kept, NCH)

            def add_exp(c, u, i):
                dve.wait_ge(exp_ready, c + 1)
                dve.tensor_tensor(relu_c[u], relu_c[u], exp_c[u], ALU.add).then_inc(elu_ready, 1)
            def finish_rows(c, u, i):
                dve.wait_ge(elu_turned, c + 1)
                dve.wait_ge(x_loaded[u], loads_done(i))
                pair = BANK_PAIR[u]
                dve.scalar_tensor_tensor(out=node_rows(c), in0=psum[0:NPART, pair * 512:pair * 512 + CW].rearrange("p (j f) -> p j f", f=D),
                                         scalar=-1.0, in1=nx[u], op0=ALU.add, op1=ALU.add).then_inc(s_ready, 1)
                dve.wait_ge(s_ready, c + 1)
                for j in range(TPN):
                    last = dve.bn_stats(st1[:, bass.ds(c * TPN + j, 1), :].rearrange("p o s -> p (o s)"), node_row(c, j))
                last.then_inc(stats1, 1)
            pipeline(dve, NCH, NSLOTS, (0, add_exp), (1, finish_rows))
            dve.wait_ge(stats1, NCH)
            me, qe, mo, qo = (st1[:, :, i] for i in (1, 2, 4, 5))
            dve.tensor_tensor(m_s, me, mo, ALU.add).then_inc(ln_small, 1)
            dve.tensor_tensor(m_d, me, mo, ALU.subtract).then_inc(ln_small, 1)
            dve.tensor_tensor(v_s, qe, qo, ALU.add).then_inc(ln_small, 1)
            dve.wait_ge(ln_small, 3)
            dve.tensor_tensor(m_d, m_d, m_d, ALU.mult).then_inc(ln_step, 1)
            dve.tensor_scalar(v_s, v_s, 1.0 / D, None, ALU.mult).then_inc(ln_step, 1)
            dve.wait_ge(ln_step, 2)
            dve.scalar_tensor_tensor(out=v_q, in0=m_d, scalar=0.25, in1=v_s, op0=ALU.mult, op1=ALU.add).then_inc(ln_step, 1)
            dve.wait_ge(ln_sqrt, 1)
            dve.reciprocal(rstd1, v_s).then_inc(ln_step, 1)
            dve.wait_ge(ln_step, 4)
            dve.scalar_tensor_tensor(out=mb1, in0=m_s, scalar=-0.5, in1=rstd1, op0=ALU.mult, op1=ALU.mult).then_inc(ln_step, 1)
            dve.wait_ge(ln_step, 5)
            with dve.Fori(0, NCH) as c:
                for j in range(ACT_NORM_FROM):
                    row = node_row(c, j)
                    a = dve.tensor_scalar(row, row, rstd1[:, bass.ds(c * TPN + j, 1)], mb1[:, bass.ds(c * TPN + j, 1)], ALU.mult, ALU.add)
                a.then_inc(norm_dve, 1)

            def step1(k, u, i):
                dve.wait_ge(L1["weight"], k + 1)
                if later(k, 1):
                    dve.wait_ge(L1["y_ready"], k)
                dve.tensor_tensor(msg, att_w, xsT, ALU.mult).then_inc(msg_ready, 1)
                dve.wait_ge(msg_ready, k + 1)
                dve.wait_ge(L1["gates"][u], loads_done(i))
                if later(k, ESLOTS):
                    dve.wait_ge(L1["y_turned"], k - ESLOTS + 1)
                dve.tensor_tensor_scan(aggT[u], gate_t[u][:, 0:CHUNK], msg,
                                       0.0 if not later(k, 1) else aggT[(u - 1) % ESLOTS][:, CHUNK - 1:CHUNK], ALU.mult, ALU.add).then_inc(L1["y_ready"], 1)
            by_width(dve, lambda narrow: pipeline(dve, EC, ESLOTS, (0, make_onehot(L1, narrow)), (2, step1)))

            def row_stats(rows, st, mv, c, u, st_sem, mv_sem):
                for j in range(TPN):
                    last = dve.bn_stats(st[:, u, j, :], rows[:, j, :])
                last.then_inc(st_sem, 1)
                dve.wait_ge(st_sem, c + 1)
                dve.nop(nofuse=True)
                for j in range(TPN):
                    last = dve.bn_aggr(mv[:, u, j, :], st[:, u, j, :])
                last.then_inc(mv_sem, 1)

            def stats_a(c, u, i):
                dve.wait_ge(n2["att"], c + 1)
                row_stats(nx[u], st2, mvA, c, u, n2["stA"], n2["mvA"])

            def scale_shift(mv, rs, mb, sd_sem, rs_sem, mb_sem):
                def stage(c, u, i):
                    dve.wait_ge(sd_sem, c + 1)
                    dve.reciprocal(rs[:, u, :], rs[:, u, :]).then_inc(rs_sem, 1)
                    dve.wait_ge(rs_sem, c + 1)
                    dve.scalar_tensor_tensor(out=mb[:, u, :], in0=mv[:, u, :, 0:1].rearrange("p j o -> p (j o)"), scalar=-1.0,
                                             in1=rs[:, u, :], op0=ALU.mult, op1=ALU.mult).then_inc(mb_sem, 1)
                return stage

            def stats_b(c, u, i):
                dve.wait_ge(n2["normA"], c + 1)
                dve.tensor_tensor(nv[u], nv[u], g1_row[:, :].unsqueeze(1).to_broadcast([NPART, TPN, D]), ALU.mult).then_inc(n2["t"], 1)
                dve.wait_ge(n2["xb"], c + 1)
                dve.wait_ge(n2["t"], c + 1)
                dve.tensor_tensor(nv[u], nv[u], ne[u], ALU.add).then_inc(n2["s"], 1)
                dve.wait_ge(n2["s"], c + 1)
                row_stats(nv[u], st3, mvB, c, u, n2["stB"], n2["mvB"])

            pipeline(dve, NCH, NSLOTS, (0, stats_a), (1, scale_shift(mvA, rsA, mbA, n2["sdA"], n2["rsA"], n2["mbA"])),
                     (2, stats_b), (3, scale_shift(mvB, rsB, mbB, n2["sdB"], n2["rsB"], n2["mbB"])))


_INS = ["x", "src", "dst", "node_vec1", "L0_gnn_W_fc", "L0_gnn_gamma", "L0_gnn_beta", "L1_gnn_W1", "L1_gnn_b1",
        "L1_gnn_W2", "L1_gnn_b2", "L1_gnn_gamma", "L1_gnn_beta"]


def kernel(**inputs):
    import numpy as _np
    import concourse.bacc as _bacc
    from concourse import mybir as _mybir
    from concourse.bass_utils import run_bass_kernel_spmd as _run

    nc = _bacc.Bacc("TRN2", target_bir_lowering=False, num_devices=1)
    arrays, args = {}, []
    for name in _INS:
        a = _np.ascontiguousarray(inputs[name])
        arrays[f"in_{name}"] = a
        args.append(nc.dram_tensor(f"in_{name}", a.shape, _mybir.dt.from_np(a.dtype), kind="ExternalInput").ap())
    out = nc.dram_tensor("out_0", inputs["x"].shape, _mybir.dt.float32, kind="ExternalOutput").ap()
    gnn_two_layers(nc, *args, out)
    r = _run(nc, [arrays], core_ids=[0])
    return r.results[0]["out_0"]
```

```python
from contextlib import ExitStack

import concourse.bass as bass
from concourse import mybir

F32 = mybir.dt.float32
BF16 = mybir.dt.bfloat16
I32 = mybir.dt.int32
FP16 = mybir.dt.float16
ALU = mybir.AluOpType
ACT = mybir.ActivationFunctionType

P = 128
EPS = 1e-5
N_CONSTS = 10
BN_STEPS = 6
X_PARTS = 5
X_FROM = 3
ZERO_FIRST = 20
ZERO_STEP = 5
BANK_PAIR = [0, 2, 4, 6, 2]
ACT_NORM_FROM = 3
LN_EXP_TABLES = 6
BIG = 1.6e38
PEELED = 3
ROWS = 125
TPC = 4
CHUNK = ROWS * TPC
ESLOTS = 3
BEHIND = 2 * ESLOTS
NPART = 120
TPN = 5
WINDOW = 4
WARM = 7
NSLOTS = 5
OUT_ROWS = 4
DVE_ROWS = 2
GAMMA_ROWS = 4
STORE_LAG = 8


def later(k, n):
    return not isinstance(k, int) or k >= n


def pipeline(eng, count, slots, *stages):
    def step(k, u, i):
        for lag, fn in stages:
            if later(k, lag) and (not isinstance(k, int) or k - lag < count):
                fn(k - lag, (u - lag) % slots, i + (u - lag) // slots)
    for k in range(PEELED * slots):
        step(k, k % slots, k // slots)
    with eng.Fori(PEELED, count // slots) as i:
        for u in range(slots):
            step(i * slots + u, u, i)
    for k in range(count, count + max(lag for lag, _ in stages)):
        step(k, k % slots, k // slots)


def loads_done(i):
    return 16 * (i + 1)


def gnn_two_layers(nc, x, src, dst, snorm, w_fc, gamma0, beta0, w1, b1, w2, b2, gamma1, beta1, out):
    N, D = x.shape
    E = src.shape[0]
    assert N == E and D == P and E % (CHUNK * ESLOTS) == 0
    EC = E // CHUNK
    ET = E // ROWS
    PER_PART = N // NPART
    NCH = PER_PART // TPN
    EROWS = E // NPART
    HALVES = EROWS // ROWS
    assert PER_PART == HALVES * ROWS and WINDOW == TPC and TPC == ESLOTS + 1
    assert HALVES == 2 and NCH % NSLOTS == 0 and PER_PART * NPART == N

    keep_dram = nc.dram_tensor("keep_scratch", (E,), BF16, kind="Internal").ap()
    gate_dram = nc.dram_tensor("gate_scratch", (E,), BF16, kind="Internal").ap()
    hout_dram = nc.dram_tensor("hout_scratch", (N, D), F32, kind="Internal").ap()
    x1_dram = nc.dram_tensor("x1_scratch", (N, D), F32, kind="Internal").ap()
    agg_dram = nc.dram_tensor("agg_scratch", (N, D), F32, kind="Internal").ap()
    rel_dram = nc.dram_tensor("rel_scratch", (E,), FP16, kind="Internal").ap()
    first_dram = nc.dram_tensor("first_scratch", (ET,), I32, kind="Internal").ap()

    def node_chunk(table, c):
        return table[bass.ds(c * TPN * NPART, TPN * NPART), :].rearrange("(j p) f -> p j f", p=NPART)

    with ExitStack() as ctx:
        def sb(name, shape, dt=F32):
            return ctx.enter_context(nc.sbuf_tensor(name, shape, dt))

        def sem(name):
            return ctx.enter_context(nc.semaphore(name))

        def sems(name, n):
            return [sem(f"{name}{i}") for i in range(n)]

        psum = ctx.enter_context(nc.psum_tensor("psum", [P, 8 * 512], F32))
        banks = [psum[:, 512 * i:512 * (i + 1)] for i in range(8)]

        CW = TPN * D
        node_table = sb("node_table", [P, NCH * CW])

        def node_cols(c):
            return node_table[:, bass.ds(c * CW, TPN * NPART)]

        def node_rows(c):
            return node_table[0:NPART, bass.ds(c * CW, CW)].rearrange("p (j f) -> p j f", f=D)

        def node_row(c, j):
            return node_table[0:NPART, bass.ds(c * CW + j * D, D)]

        ARENA = 18270
        arena = sb("arena", [P, ARENA])

        def carve(sizes, at=0):
            views = []
            for n in sizes:
                views.append(arena[:, at:at + n])
                at += n
            assert at <= ARENA, at
            return views

        SRC, DST, END = range(3)
        idx_all = sb("idx_all", [P, EC + BEHIND, 3, TPC], I32)
        idx_now = sb("idx_now", [P, ESLOTS, 3, TPC], I32)
        ident = sb("ident", [P, P])
        w_fc_sb = sb("w_fc_sb", [P, P])
        w_fcT = sb("w_fcT", [P, P])
        w1_sb = sb("w1_sb", [P, 2, P])
        w2_col = sb("w2_col", [P, 1])
        w2_wide = sb("w2_wide", [P, P])
        cols = sb("cols", [P, 16])
        b1_col, b2_col, g0_col, be0_col = (cols[:, i:i + 1] for i in range(4))
        eps_col, sd_col, rs_col, a_col, ma_col, b_col, na_col, nb_col = (cols[:, i:i + 1] for i in range(4, 12))
        mv0 = cols[:, 12:14]
        g1_row = sb("g1_row", [NPART, D])
        be1_row = sb("be1_row", [NPART, D])
        snorm_sb = sb("snorm_sb", [NPART, PER_PART])
        first_row = sb("first_row", [1, ET], I32)
        flag = sb("flag", [1, 1], I32)
        flag_f = sb("flag_f", [1, 1])
        win_i = sb("win_i", [NPART, WINDOW], I32)
        win_f = sb("win_f", [NPART, WINDOW])
        tcol = [sb(f"tcol{i}", [NPART, HALVES]) for i in range(7)]
        tcol_i = [sb(f"tcol_i{i}", [NPART, HALVES], I32) for i in range(2)]
        rel_max = sb("rel_max", [NPART, 1])

        HSLOTS = 3
        HALF_CHUNK = CHUNK // 2
        A = carve([EROWS] * 12, ARENA - HSLOTS * WINDOW * HALF_CHUNK - WINDOW * D)
        snorm_in = A[10][0:ROWS, 0:HALVES * NPART].rearrange("p (h q) -> p h q", h=HALVES)
        rel_f = A[9][0:NPART]
        rel_h = A[11][0:NPART].bitcast(FP16)[:, 0:EROWS]
        src_i, dst_i, nxt_i, prv_i = (a[0:NPART].bitcast(I32) for a in A[0:4])
        src_f, dst_f, same_f, end_f = (a[0:NPART] for a in A[4:8])
        bf = A[8][0:NPART].bitcast(BF16)
        keep_b, gate_b = bf[:, 0:EROWS], bf[:, EROWS:2 * EROWS]
        ZER = max(TPN, TPC) * D
        V = carve([TPC * D] * 9 + [CHUNK] * 11 + [CHUNK + 1] + [CHUNK // 2] * 2 * ESLOTS + [ZER] + [WINDOW * HALF_CHUNK] * HSLOTS + [WINDOW * D])
        rows_s = [v.rearrange("p (t f) -> p t f", f=D) for v in V[0:3]]
        rows_d = [v.rearrange("p (t f) -> p t f", f=D) for v in V[3:6]]
        rows_y = [v.rearrange("p (t f) -> p t f", f=D) for v in V[6:9]]
        xsT, xdT, zsT, e_t, delta, c_t, ex_t, den, num, y_t, rec_t = V[9:20]
        gmax = V[20]
        hid, att_w, msg = V[11:14]
        aggT = V[14:17]
        gate_t = [v.bitcast(BF16) for v in V[21:24]]
        rel_t = [v[0:NPART].bitcast(FP16) for v in V[24:27]]
        zeros = V[27]
        onehot = [v[0:NPART].rearrange("p (w e) -> p w e", w=WINDOW) for v in V[28:31]]
        window = [v[0:NPART] for v in V[3:6] + V[31:32]]
        NV = carve([TPN * D] * (4 * NSLOTS) + [2 * NCH * 6] + [NSLOTS * TPN * 6] * 2 + [NSLOTS * TPN * 2] * 2 + [NSLOTS * TPN] * 4)
        relu_c, exp_c = ([v[:, 0:TPN * NPART] for v in NV[NSLOTS * i:NSLOTS * (i + 1)]] for i in (1, 2))
        nview = [v[0:NPART].rearrange("p (j f) -> p j f", f=D) for v in NV[0:4 * NSLOTS]]
        nx, nv, ne, no = (nview[NSLOTS * i:NSLOTS * (i + 1)] for i in range(4))
        st0 = NV[20].rearrange("p (c s) -> p c s", s=6)
        stA, stB = (v[0:NPART].rearrange("p (u j s) -> p u j s", u=NSLOTS, s=6) for v in NV[21:23])
        mvA, mvB = (v[0:NPART].rearrange("p (u j s) -> p u j s", u=NSLOTS, s=2) for v in NV[23:25])
        rsA, mbA, rsB, mbB = (v[0:NPART].rearrange("p (u j) -> p u j", u=NSLOTS) for v in NV[25:29])
        carry = sb("carry", [P, 2])
        eps_n = sb("eps_n", [NPART, 1])

        consts = sem("consts")
        edges_loaded = sem("edges_loaded")
        minus_one = sem("minus_one")
        shifted = sem("shifted")
        ident_zero = sem("ident_zero")
        ident_ready = sem("ident_ready")
        small = sem("small")
        tables = sem("tables")
        idx_turned = sem("idx_turned")
        idx_ready = sem("idx_ready")
        gates_stored = sem("gates_stored")
        zeros_ready = sem("zeros_ready")
        hout_zeroed = sem("hout_zeroed")
        agg_zeroed = sem("agg_zeroed")

        first_step = sem("first_step")
        rel_ready = sem("rel_ready")
        first_stored = sem("first_stored")
        first_ready = sem("first_ready")
        max_turned = sem("max_turned")
        flag_step = sem("flag_step")
        win_ready = sem("win_ready")
        snorm_ready = sem("snorm_ready")
        sums_carried = sem("sums_carried")
        x_resident = sem("x_resident")

        block = ctx.enter_context(nc.Block())

        def by_width(eng, edge_pass):
            is_narrow = eng.value_load(flag[0:1, 0:1], min_val=0, max_val=1)
            with eng.If(is_narrow == 1):
                edge_pass(True)
            with eng.Else():
                edge_pass(False)

        def gathers_dst(L, k, narrow):
            return not narrow or (L is L0 and isinstance(k, int) and k < WARM)

        def edge_sems(n):
            return dict(
                gathered=sems(f"gathered{n}_", ESLOTS), gates=sems(f"gates{n}_", ESLOTS),
                scattered=sems(f"scattered{n}_", ESLOTS), staged=sem(f"staged{n}"),
                turned=sem(f"turned{n}"), copied=sem(f"copied{n}"), product=sem(f"product{n}"),
                zs_copied=sem(f"zs_copied{n}"), weight=sem(f"weight{n}"), y_turned=sem(f"y_turned{n}"),
                y_rows=sem(f"y_rows{n}"), y_ready=sem(f"y_ready{n}"), logit=sem(f"logit{n}"),
                rel=sems(f"rel{n}_", ESLOTS), onehot=sem(f"onehot{n}"), window_copied=sem(f"window_copied{n}"), window_used=sem(f"window_used{n}"))
        L0, L1 = edge_sems(0), edge_sems(1)
        e_ready, carry_ready, gmax_ready, delta_ready = (sem(s) for s in ("e_ready", "carry_ready", "gmax_ready", "delta_ready"))
        act_step, exps_ready, w_ready, den_ready, num_ready = (sem(s) for s in ("act_step", "exps_ready", "w_ready", "den_ready", "num_ready"))
        rec_ready, ln_ready = sem("rec_ready"), sem("ln_ready")
        msg_ready = sem("msg_ready")
        hout_loaded = sems("hout_loaded", NSLOTS)
        kept = sem("kept")
        scaled, scaled_rest, node_turned, stats0 = sem("scaled"), sem("scaled_rest"), sem("node_turned"), sem("stats0")
        bn_step, bn_log, bn_root = sem("bn_step"), sem("bn_log"), sem("bn_root")
        x_loaded = sems("x_loaded", NSLOTS)
        neg_ready, exp_ready, elu_ready, elu_turned, s_ready = (
            sem(s) for s in ("neg_ready", "exp_ready", "elu_ready", "elu_turned", "s_ready"))
        norm_dve, norm_act = sem("norm_dve"), sem("norm_act")
        n1 = {s: sem("n1_" + s) for s in ("st", "mv", "log", "rs", "mb")}
        x1_stored = sem("x1_stored")
        agg_loaded = sems("agg_loaded", NSLOTS)
        out_stored = sems("out_stored", NSLOTS)
        n2 = {s: sem("n2_" + s) for s in ("att", "xb", "t", "t_rest", "s", "stA", "mvA", "sdA", "rsA", "mbA", "normA", "stB", "mvB", "sdB", "rsB", "mbB", "normB", "normB_rest")}

        @block.sync
        def _(sp):
            col = lambda v: v.rearrange("(p o) -> p o", o=1)
            loads = [(w_fc_sb[:, :], w_fc), (w1_sb[:, :, :], w1.rearrange("(a k) h -> k a h", a=2)),
                     (w2_col[:, :], w2), (b1_col, col(b1)), (b2_col, b2.partition_broadcast(P)),
                     (g0_col, col(gamma0)), (be0_col, col(beta0)),
                     (g1_row[:, :], gamma1.partition_broadcast(NPART)),
                     (be1_row[:, :], beta1.partition_broadcast(NPART)),
                     (snorm_in[:, :, :], snorm.rearrange("(q h p) o -> q h (p o)", h=HALVES, p=NPART))]
            assert len(loads) == N_CONSTS
            sp.dma_start(dst_i, dst.rearrange("(p j) -> p j", p=NPART)).then_inc(edges_loaded, 16)
            sp.dma_start(src_i, src.rearrange("(p j) -> p j", p=NPART)).then_inc(edges_loaded, 16)
            sp.wait_ge(minus_one, 1)
            last = (NPART - 1) * EROWS
            sp.dma_start(nxt_i[0:NPART - 1, :], dst[1:last + 1].rearrange("(p j) -> p j", j=EROWS)).then_inc(shifted, 16)
            sp.dma_start(nxt_i[NPART - 1:NPART, 0:EROWS - 1], dst[last + 1:E].rearrange("(p j) -> p j", p=1)).then_inc(shifted, 16)
            sp.dma_start(prv_i[0:1, 1:EROWS], dst[0:EROWS - 1].rearrange("(p j) -> p j", p=1)).then_inc(shifted, 16)
            sp.dma_start(prv_i[1:NPART, :], dst[EROWS - 1:E - 1].rearrange("(p j) -> p j", j=EROWS)).then_inc(shifted, 16)
            for to, fr in loads:
                sp.dma_start(to, fr).then_inc(consts, 16)
            sp.wait_ge(tables, 5)
            sp.dma_start(keep_dram.rearrange("(p j) -> p j", p=NPART), keep_b).then_inc(gates_stored, 16)
            sp.dma_start(gate_dram.rearrange("(p j) -> p j", p=NPART), gate_b).then_inc(gates_stored, 16)
            sp.wait_ge(rel_ready, 3)
            sp.dma_start(rel_dram.rearrange("(p j) -> p j", p=NPART), rel_h).then_inc(gates_stored, 16)
            sp.dma_start(first_dram.rearrange("(q h) -> q h", h=HALVES), tcol_i[1][:, :]).then_inc(first_stored, 16)
            sp.wait_ge(first_stored, 16)
            sp.dma_start(first_row[:, :], first_dram.rearrange("(o t) -> o t", o=1)).then_inc(first_ready, 16)
            sp.wait_ge(gates_stored, 48)

            sp.wait_ge(zeros_ready, 1)
            def gate_load(L, table, used, narrow):
                def step(k, u, i):
                    if narrow:
                        if later(k, ESLOTS):
                            sp.wait_ge(L["onehot"], 2 * (k - ESLOTS + 1))
                            sp.nop(nofuse=True)
                        sp.dma_start(rel_t[u], rel_dram[bass.ds(k * CHUNK, CHUNK)].partition_broadcast(NPART)).then_inc(L["rel"][u], 16)
                    if later(k, ESLOTS):
                        sp.wait_ge(used, k - ESLOTS + 1)
                        sp.nop(nofuse=True)
                    sp.dma_start(gate_t[u][:, 0:CHUNK], table[bass.ds(k * CHUNK, CHUNK)].partition_broadcast(P)).then_inc(L["gates"][u], 16)
                    if narrow and L is L0 and isinstance(k, int) and X_FROM <= k < X_FROM + X_PARTS:
                        c, w = k - X_FROM, PER_PART // X_PARTS
                        sp.dma_start(node_table[0:NPART, c * w * D:(c + 1) * w * D].rearrange("p (t f) -> p t f", f=D),
                                     x[c * w * NPART:(c + 1) * w * NPART, :].rearrange("(t p) f -> p t f", p=NPART)).then_inc(x_resident, 16)
                return step
            def zero_sums(k, u, i):
                sp.dma_start(agg_dram[bass.ds(k * CHUNK, CHUNK), :].rearrange("(p t) f -> p (t f)", t=TPN),
                             zeros[0:CHUNK // TPN, 0:CW]).then_inc(agg_zeroed, 16)
            sp.wait_ge(flag_step, 2)
            by_width(sp, lambda narrow: pipeline(sp, EC, ESLOTS, (0, gate_load(L0, gate_dram, gmax_ready, narrow)), (WARM + 2, zero_sums)))

            for u in range(ESLOTS):
                sp.wait_ge(L0["scattered"][u], 16 * TPC * (EC // ESLOTS))
            def hout_load(c, u, i):
                if later(c, NSLOTS):
                    sp.wait_ge(scaled, c - NSLOTS + 1)
                    sp.wait_ge(scaled_rest, c - NSLOTS + 1)
                sp.dma_start(nx[u], node_chunk(hout_dram, c)).then_inc(hout_loaded[u], 16)
            pipeline(sp, NCH, NSLOTS, (0, hout_load))
            def x_load(c, u, i):
                if later(c, NSLOTS):
                    sp.wait_ge(s_ready, c - NSLOTS + 1)
                sp.dma_start(nx[u], node_chunk(x, c)).then_inc(x_loaded[u], 16)
            sp.wait_ge(scaled, NCH)
            sp.wait_ge(scaled_rest, NCH)
            def x1_store(c, u, i):
                sp.wait_ge(norm_dve, c + 1)
                sp.wait_ge(norm_act, c + 1)
                sp.dma_start(node_chunk(x1_dram, c), node_rows(c)).then_inc(x1_stored, 16)
            pipeline(sp, NCH, NSLOTS, (0, x_load), (STORE_LAG, x1_store))

            by_width(sp, lambda narrow: pipeline(sp, EC, ESLOTS, (0, gate_load(L1, keep_dram, L1["y_ready"], narrow))))

            for u in range(ESLOTS):
                sp.wait_ge(L1["scattered"][u], 16 * TPC * (EC // ESLOTS))
            def agg_load(c, u, i):
                if later(c, NSLOTS):
                    sp.wait_ge(n2["normA"], c - NSLOTS + 1)
                sp.dma_start(nx[u], node_chunk(agg_dram, c)).then_inc(agg_loaded[u], 16)
            def out_store(c, u, i):
                sp.wait_ge(n2["normB"], c + 1)
                sp.wait_ge(n2["normB_rest"], c + 1)
                sp.dma_start(node_chunk(out, c), no[u]).then_inc(out_stored[u], 16)
            pipeline(sp, NCH, NSLOTS, (0, agg_load), (STORE_LAG, out_store))
            for u in range(NSLOTS):
                sp.wait_ge(out_stored[u], 16 * (NCH // NSLOTS))

        @block.gpsimd
        def _(pool):
            pool.memset(nxt_i, -1)
            pool.memset(prv_i, -1).then_inc(minus_one, 1)
            pool.memset(zeros, 0.0).then_inc(zeros_ready, 1)
            pool.memset(ident[:, :], 0.0).then_inc(ident_zero, 1)
            pool.wait_ge(ident_zero, 1)
            pool.affine_select(out=ident[:, :], in_=ident[:, :], compare_op=ALU.not_equal, fill=1.0, base=0,
                               pattern=[[-1, P]], channel_multiplier=1).then_inc(ident_ready, 1)

            pool.iota(win_i[:, :], pattern=[[NPART, WINDOW]], base=0, channel_multiplier=1).then_inc(win_ready, 1)

            def gather(L, table, k, u, i, narrow):
                if later(k, ESLOTS):
                    pool.wait_ge(L["turned"], k - ESLOTS + 1)
                    pool.nop(nofuse=True)
                if later(k, BEHIND + ESLOTS):
                    pool.wait_ge(L["scattered"][u], (i - BEHIND // ESLOTS) * 16 * TPC)
                pool.tensor_copy(idx_now[0:ROWS, u, :, :],
                                 idx_all[0:ROWS, bass.ds(k, 1), :, :].rearrange("r o n t -> r (o n) t")).then_inc(L["staged"], 1)
                pool.wait_ge(L["staged"], k + 1)
                pool.nop(nofuse=True)
                ends = [(SRC, rows_s)] + [(DST, rows_d)] * gathers_dst(L, k, narrow)
                for t in range(TPC):
                    for n, rows in ends:
                        pool.indirect_dma_start(
                            out=rows[u][0:ROWS, t, :], out_offset=None, in_=table,
                            in_offset=bass.IndirectOffsetOnAxis(ap=idx_now[0:ROWS, u, n, t:t + 1], axis=0),
                        ).then_inc(L["gathered"][u], 16)

            def scatter(L, table, k, u):
                pool.wait_ge(L["y_rows"], k + 1)
                pool.nop(nofuse=True)
                for t in range(TPC):
                    pool.indirect_dma_start(
                        out=table, out_offset=bass.IndirectOffsetOnAxis(ap=idx_now[0:ROWS, u, END, t:t + 1], axis=0),
                        in_=rows_y[u][0:ROWS, t, :], in_offset=None, bounds_check=N - 1, oob_is_err=False,
                    ).then_inc(L["scattered"][u], 16)

            def edge_pass(L, table, result, zeroed, chunks, narrow):
                for k in range(PEELED * ESLOTS):
                    gather(L, table, k, k % ESLOTS, k // ESLOTS, narrow)
                    if k == BEHIND:
                        pool.wait_ge(zeroed, 16 * chunks)
                    if k >= BEHIND:
                        scatter(L, result, k - BEHIND, k % ESLOTS)
                with pool.Fori(PEELED, EC // ESLOTS) as i:
                    for u in range(ESLOTS):
                        gather(L, table, i * ESLOTS + u, u, i, narrow)
                        scatter(L, result, i * ESLOTS + u - BEHIND, u)
                for k in range(EC, EC + BEHIND):
                    u = k % ESLOTS
                    pool.wait_ge(L["scattered"][u], (k // ESLOTS - BEHIND // ESLOTS) * 16 * TPC)
                    pool.tensor_copy(idx_now[0:ROWS, u, END, :], idx_all[0:ROWS, k, END, :]).then_inc(L["staged"], 1)
                    pool.wait_ge(L["staged"], k + 1)
                    scatter(L, result, k - BEHIND, u)

            pool.wait_ge(idx_ready, 3)
            pool.wait_ge(flag_step, 2)
            by_width(pool, lambda narrow: edge_pass(L0, x, hout_dram, hout_zeroed, NCH, narrow))
            def scale_rest(c, u, i):
                pool.wait_ge(hout_loaded[u], loads_done(i))
                if later(c, NSLOTS):
                    pool.wait_ge(node_turned, c - NSLOTS + 1)
                pool.nop(nofuse=True)
                pool.tensor_tensor(nv[u][:, DVE_ROWS:TPN, :], nx[u][:, DVE_ROWS:TPN, :],
                                   snorm_sb[:, bass.ds(c * TPN + DVE_ROWS, TPN - DVE_ROWS)].unsqueeze(2).to_broadcast([NPART, TPN - DVE_ROWS, D]),
                                   ALU.mult).then_inc(scaled_rest, 1)
            pipeline(pool, NCH, NSLOTS, (0, scale_rest))
            def add_exp(c, u, i):
                pool.wait_ge(exp_ready, c + 1)
                pool.tensor_tensor(relu_c[u], relu_c[u], exp_c[u], ALU.add).then_inc(elu_ready, 1)
            pipeline(pool, NCH, NSLOTS, (0, add_exp))
            pool.wait_ge(x1_stored, 16 * NCH)
            by_width(pool, lambda narrow: edge_pass(L1, x1_dram, agg_dram, agg_zeroed, EC, narrow))

            def add_rows(c, u, i):
                pool.wait_ge(agg_loaded[u], loads_done(i))
                pool.nop(nofuse=True)
                pool.tensor_tensor(nx[u], nx[u], node_rows(c), ALU.add).then_inc(n2["att"], 1)
                if later(c, NSLOTS):
                    pool.wait_ge(n2["s"], c - NSLOTS + 1)
                    pool.nop(nofuse=True)
                pool.tensor_tensor(ne[u], node_rows(c), be1_row[:, :].unsqueeze(1).to_broadcast([NPART, TPN, D]), ALU.add).then_inc(n2["xb"], 1)
            def times_gamma(c, u, i):
                pool.wait_ge(n2["normA"], c + 1)
                pool.nop(nofuse=True)
                pool.tensor_tensor(nv[u][:, 0:GAMMA_ROWS, :], nv[u][:, 0:GAMMA_ROWS, :],
                                   g1_row[:, :].unsqueeze(1).to_broadcast([NPART, GAMMA_ROWS, D]), ALU.mult).then_inc(n2["t"], 1)
            pipeline(pool, NCH, NSLOTS, (0, add_rows), (2, times_gamma))

        @block.tensor
        def _(pe):
            pe.wait_ge(ident_ready, 1)
            pe.wait_ge(tables, 3)
            for n, tab in enumerate((src_f, dst_f, end_f)):
                for h in range(HALVES):
                    mm = pe.transpose(banks[n][0:ROWS, h * NPART:(h + 1) * NPART],
                                      tab[:, h * ROWS:(h + 1) * ROWS], ident[0:NPART, 0:NPART])
                mm.then_inc(idx_turned, 1)
            pe.wait_ge(rel_ready, 4)
            pe.transpose(banks[4][0:1, 0:NPART], rel_max[:, :], ident[0:NPART, 0:NPART]).then_inc(max_turned, 1)
            pe.wait_ge(consts, 16 * N_CONSTS)
            pe.transpose(banks[3][:, 0:P], w_fc_sb[:, :], ident[:, :]).then_inc(idx_turned, 1)
            for h in range(HALVES):
                mm = pe.transpose(banks[5][0:NPART, h * ROWS:(h + 1) * ROWS], snorm_in[:, h, :], ident[0:ROWS, 0:ROWS])
            mm.then_inc(max_turned, 1)

            def expand(L, narrow):
                def stage(k, u, i):
                    if not narrow:
                        return
                    if gathers_dst(L, k, narrow):
                        pe.nop(nofuse=True).then_inc(L["window_used"], TPC)
                        return
                    if later(k, ESLOTS):
                        pe.wait_ge(L["copied"], k - ESLOTS + 1)
                    for t in range(TPC):
                        half, e = divmod(t * ROWS, HALF_CHUNK)
                        if e == 0:
                            pe.wait_ge(L["onehot"], 2 * k + half + 1)
                        pe.wait_ge(L["window_copied"], k * TPC + t + 1)
                        for w in range(WINDOW):
                            mm = pe.matmul(banks[5 + u][:, t * ROWS:(t + 1) * ROWS], window[t][:, w * D:(w + 1) * D],
                                           onehot[(2 * u + half) % HSLOTS][:, w, e:e + ROWS], start=(w == 0), stop=(w == WINDOW - 1))
                        mm.then_inc(L["window_used"], 1)
                return stage

            def turn(L, narrow):
                def stage(k, u, i):
                    both = gathers_dst(L, k, narrow)
                    if both:
                        pe.wait_ge(L["gathered"][u], (i + 1) * 32 * TPC)
                    else:
                        warm = len(range(u, WARM, ESLOTS)) if L is L0 else 0
                        pe.wait_ge(L["gathered"][u], (i + 1 + warm) * 16 * TPC)
                    if later(k, 1):
                        pe.wait_ge(L["copied"], k)
                    for bank, rows in ((0, rows_s), (1, rows_d))[:1 + both]:
                        for t in range(TPC):
                            mm = pe.transpose(banks[bank][:, t * ROWS:(t + 1) * ROWS], rows[u][0:ROWS, t, :], ident[0:ROWS, 0:ROWS])
                    mm.then_inc(L["turned"], 1)
                return stage

            def turn_back(L, ys):
                def stage(k, u, i):
                    pe.wait_ge(L["y_ready"], k + 1)
                    if later(k, 1):
                        pe.wait_ge(L["y_rows"], k)
                    for t in range(TPC):
                        mm = pe.transpose(banks[4][0:ROWS, t * D:(t + 1) * D], ys[u][:, t * ROWS:(t + 1) * ROWS], ident[:, :])
                    mm.then_inc(L["y_turned"], 1)
                return stage

            def products0(k, u, i):
                pe.wait_ge(L0["copied"], k + 1)
                if later(k, 1):
                    pe.wait_ge(L0["zs_copied"], k)
                    pe.wait_ge(e_ready, k)
                pe.matmul(banks[2][:, 0:CHUNK], w_fcT[:, :], xsT, start=True, stop=True)
                pe.matmul(banks[3][:, 0:CHUNK], w_fcT[:, :], xdT, start=True, stop=True).then_inc(L0["product"], 1)
            pe.wait_ge(idx_ready, 5)
            pe.wait_ge(flag_step, 2)
            pe.wait_ge(first_ready, 16)
            by_width(pe, lambda narrow: pipeline(pe, EC, ESLOTS, (2, products0), (4, turn_back(L0, [y_t] * ESLOTS)),
                                                 (1, turn(L0, narrow)), (1, expand(L0, narrow))))

            def turn_nodes(c, u, i):
                pe.wait_ge(scaled, c + 1)
                pe.wait_ge(scaled_rest, c + 1)
                if later(c, 2):
                    pe.wait_ge(kept, c - 1)
                pair = BANK_PAIR[u]
                for j in range(TPN):
                    mm = pe.transpose(banks[pair + j // 3][:, (j % 3) * NPART:(j % 3 + 1) * NPART],
                                      nv[u][:, j, :], ident[0:NPART, 0:NPART])
                mm.then_inc(node_turned, 1)
            pe.wait_ge(L0["y_rows"], EC)
            pipeline(pe, NCH, NSLOTS, (0, turn_nodes))
            def turn_elu(c, u, i):
                pe.wait_ge(elu_ready, c + 1)
                if later(c, 2):
                    pe.wait_ge(s_ready, c - 1)
                pair = BANK_PAIR[u]
                for j in range(TPN):
                    at = pair * 512 + j * D
                    mm = pe.transpose(psum[0:NPART, at:at + D], relu_c[u][:, j * NPART:(j + 1) * NPART], ident[:, :])
                mm.then_inc(elu_turned, 1)
            pipeline(pe, NCH, NSLOTS, (0, turn_elu))

            def hidden1(k, u, i):
                pe.wait_ge(L1["copied"], k + 1)
                if later(k, 1):
                    pe.wait_ge(L1["zs_copied"], k)
                pe.matmul(banks[2][:, 0:CHUNK], w1_sb[:, 0, :], xsT, start=True, stop=False)
                pe.matmul(banks[2][:, 0:CHUNK], w1_sb[:, 1, :], xdT, start=False, stop=True).then_inc(L1["product"], 1)
            def logit1(k, u, i):
                pe.wait_ge(L1["zs_copied"], k + 1)
                if later(k, 1):
                    pe.wait_ge(L1["weight"], k)
                pe.matmul(banks[3][:, 0:CHUNK], w2_wide[:, :], hid, start=True, stop=True).then_inc(L1["logit"], 1)
            pe.wait_ge(s_ready, NCH)
            by_width(pe, lambda narrow: pipeline(pe, EC, ESLOTS, (2, hidden1), (3, turn_back(L1, aggT)), (1, turn(L1, narrow)),
                                                 (2, logit1), (1, expand(L1, narrow))))

        @block.scalar
        def _(act):
            act.wait_ge(zeros_ready, 1)
            def zero_hout(first, last):
                if first < min(last, NCH):
                    with act.Fori(first, min(last, NCH)) as c:
                        act.dma_start(hout_dram[bass.ds(c * TPN * NPART, TPN * NPART), :].rearrange("(p j) f -> p (j f)", j=TPN),
                                      zeros[0:NPART, 0:CW]).then_inc(hout_zeroed, 16)
            zero_hout(0, ZERO_FIRST)
            def zero_rows(k, u, i):
                if isinstance(k, int):
                    zero_hout(ZERO_FIRST + k * ZERO_STEP, ZERO_FIRST + (k + 1) * ZERO_STEP)

            def copy_windows(L, narrow):
                def stage(k, u, i):
                    if not narrow:
                        return
                    if gathers_dst(L, k, narrow):
                        act.nop(nofuse=True).then_inc(L["window_copied"], TPC)
                        return
                    if L is L0 and isinstance(k, int) and k == WARM:
                        act.wait_ge(L["turned"], WARM)
                        act.wait_ge(x_resident, 16 * X_PARTS)
                    _, firsts = nc.values_load_multi_w_load_instructions(
                        first_row[0:1, bass.ds(k * TPC, TPC)], engines=(mybir.EngineType.Activation,), min_val=0, max_val=PER_PART - WINDOW,
                        skip_runtime_bounds_check_because="VectorE bounds it")
                    for t, first in enumerate(firsts):
                        if later(k, 1):
                            act.wait_ge(L["window_used"], (k - 1) * TPC + t + 1)
                            act.nop(nofuse=True)
                        act.copy(window[t], node_table[0:NPART, bass.ds(first * D, WINDOW * D)]).then_inc(L["window_copied"], 1)
                return stage

            def copy_in(L, free, narrow):
                def stage(k, u, i):
                    act.wait_ge(L["turned"], k + 1)
                    if later(k, 1):
                        act.wait_ge(free, k)
                    act.copy(xsT, banks[0][:, 0:CHUNK])
                    if not gathers_dst(L, k, narrow):
                        act.wait_ge(L["window_used"], (k + 1) * TPC)
                    act.copy(xdT, banks[1 if gathers_dst(L, k, narrow) else 5 + u][:, 0:CHUNK]).then_inc(L["copied"], 1)
                return stage

            def copy_rows(L):
                def stage(k, u, i):
                    act.wait_ge(L["y_turned"], k + 1)
                    if later(k, ESLOTS):
                        act.wait_ge(L["scattered"][u], i * 16 * TPC)
                    act.copy(rows_y[u][0:ROWS], banks[4][0:ROWS, :].rearrange("p (t f) -> p t f", f=D)).then_inc(L["y_rows"], 1)
                return stage

            def copy_zs(k, u, i):
                act.wait_ge(L0["product"], k + 1)
                if later(k, 1):
                    act.wait_ge(w_ready, k)
                act.copy(zsT, banks[2][:, 0:CHUNK]).then_inc(L0["zs_copied"], 1)

            def reciprocal0(k, u, i):
                act.wait_ge(den_ready, k + 1)
                if later(k, 1):
                    act.wait_ge(L0["y_ready"], k)
                act.activation(rec_t, den, ACT.Ln).then_inc(ln_ready, 1)
                act.wait_ge(ln_ready, k + 1)
                act.activation(rec_t, rec_t, ACT.Exp, scale=-1.0).then_inc(rec_ready, 1)

            def exps0(k, u, i):
                act.wait_ge(delta_ready, k + 1)
                if later(k, 1):
                    act.wait_ge(num_ready, k)
                act.activation(c_t, delta, ACT.Relu).then_inc(act_step, 1)
                act.activation(ex_t, delta, ACT.Relu, scale=-1.0).then_inc(act_step, 1)
                act.wait_ge(act_step, 2 * k + 2)
                act.activation(c_t, c_t, ACT.Exp, scale=-1.0)
                act.activation(ex_t, ex_t, ACT.Exp, scale=-1.0).then_inc(exps_ready, 1)
            act.wait_ge(flag_step, 2)
            act.wait_ge(first_ready, 16)
            act.add_instruction(mybir.InstLoadActFuncSet(name=nc.get_next_instruction_name(), act_func_set_id=LN_EXP_TABLES,
                                                         engine=mybir.EngineType.Activation))
            by_width(act, lambda narrow: pipeline(act, EC, ESLOTS, (0, zero_rows), (2, copy_zs), (3, reciprocal0), (4, copy_rows(L0)), (2, exps0),
                                                  (1, copy_in(L0, L0["product"], narrow)), (0, copy_windows(L0, narrow))))

            def keep_cols(c, u, i):
                act.wait_ge(node_turned, c + 1)
                pair = BANK_PAIR[u]
                act.copy(node_table[:, bass.ds(c * CW, 3 * NPART)], banks[pair][:, 0:3 * NPART])
                act.copy(node_table[:, bass.ds(c * CW + 3 * NPART, 2 * NPART)], banks[pair + 1][:, 0:2 * NPART]).then_inc(kept, 1)
            pipeline(act, NCH, NSLOTS, (0, keep_cols))
            act.wait_ge(bn_step, 1)
            act.activation(sd_col, mv0[:, 1:2], ACT.Ln, bias=eps_col).then_inc(bn_log, 1)
            act.wait_ge(bn_log, 1)
            act.activation(rs_col, sd_col, ACT.Exp, scale=-0.5).then_inc(bn_root, 1)
            act.wait_ge(bn_step, BN_STEPS)
            def elu(c, u, i):
                if later(c, NSLOTS):
                    act.wait_ge(elu_turned, c - NSLOTS + 1)
                act.activation(exp_c[u], node_cols(c), ACT.Relu, scale=na_col, bias=nb_col).then_inc(neg_ready, 1)
                act.activation(relu_c[u], node_cols(c), ACT.Relu, scale=a_col, bias=b_col)
                act.wait_ge(neg_ready, c + 1)
                act.activation(exp_c[u], exp_c[u], ACT.Exp, scale=-1.0).then_inc(exp_ready, 1)

            def root(mv, rs, ready, log_done, done):
                def stage(c, u, i):
                    act.wait_ge(ready, c + 1)
                    act.activation(rs[:, u, :], mv[:, u, :, 1:2].rearrange("p j o -> p (j o)"), ACT.Ln, bias=eps_n[:, :]).then_inc(log_done, 1)
                    act.wait_ge(log_done, c + 1)
                    act.activation(rs[:, u, :], rs[:, u, :], ACT.Exp, scale=-0.5).then_inc(done, 1)
                return stage
            def norm_x1(c, u, i):
                act.wait_ge(n1["mb"], c + 1)
                for j in range(ACT_NORM_FROM, TPN):
                    row = node_row(c, j)
                    a = act.activation(row, row, ACT.Identity, bias=mbA[:, u, j:j + 1], scale=rsA[:, u, j:j + 1])
                a.then_inc(norm_act, 1)
            pipeline(act, NCH, NSLOTS, (0, elu), (2, root(mvA, rsA, n1["mv"], n1["log"], n1["rs"])), (4, norm_x1))

            def relu1(k, u, i):
                act.wait_ge(L1["product"], k + 1)
                if later(k, 1):
                    act.wait_ge(L1["logit"], k)
                act.activation(hid, banks[2][:, 0:CHUNK], ACT.Relu, bias=b1_col).then_inc(L1["zs_copied"], 1)
            def sigmoid1(k, u, i):
                act.wait_ge(L1["logit"], k + 1)
                if later(k, 1):
                    act.wait_ge(msg_ready, k)
                act.activation(att_w, banks[3][:, 0:CHUNK], ACT.Sigmoid, bias=b2_col).then_inc(L1["weight"], 1)
            act.wait_ge(x1_stored, 16 * NCH)
            by_width(act, lambda narrow: pipeline(act, EC, ESLOTS, (2, relu1), (3, copy_rows(L1)), (2, sigmoid1), (1, copy_in(L1, msg_ready, narrow)),
                                                  (0, copy_windows(L1, narrow))))

            def deviation(mv, sd, ready, done):
                def stage(c, u, i):
                    act.wait_ge(ready, c + 1)
                    act.activation(sd[:, u, :], mv[:, u, :, 1:2].rearrange("p j o -> p (j o)"), ACT.Sqrt, bias=eps_n[:, :]).then_inc(done, 1)
                return stage
            def norm_a(c, u, i):
                act.wait_ge(n2["mbA"], c + 1)
                if later(c, NSLOTS):
                    act.wait_ge(n2["normB"], c - NSLOTS + 1)
                    act.wait_ge(n2["normB_rest"], c - NSLOTS + 1)
                for j in range(TPN):
                    last = act.activation(nv[u][:, j, :], nx[u][:, j, :], ACT.Identity, bias=mbA[:, u, j:j + 1], scale=rsA[:, u, j:j + 1])
                last.then_inc(n2["normA"], 1)
            def norm_b(c, u, i):
                act.wait_ge(n2["mbB"], c + 1)
                if later(c, NSLOTS):
                    act.wait_ge(out_stored[u], 16 * i)
                for j in range(OUT_ROWS):
                    last = act.activation(no[u][:, j, :], nv[u][:, j, :], ACT.Identity, bias=mbB[:, u, j:j + 1], scale=rsB[:, u, j:j + 1])
                last.then_inc(n2["normB"], 1)
            pipeline(act, NCH, NSLOTS, (0, deviation(mvA, rsA, n2["mvA"], n2["sdA"])), (1, norm_a),
                     (4, deviation(mvB, rsB, n2["mvB"], n2["sdB"])), (5, norm_b))

        @block.vector
        def _(dve):
            dve.memset(idx_all[:, 0:BEHIND, END, :], 0)
            dve.memset(eps_col, EPS)
            dve.memset(eps_n[:, :], EPS)
            dve.wait_ge(edges_loaded, 32)
            dve.wait_ge(shifted, 64)
            dve.tensor_copy(src_f, src_i).then_inc(tables, 1)
            dve.tensor_copy(dst_f, dst_i).then_inc(tables, 1)
            dve.tensor_tensor(same_f, dst_i, nxt_i, ALU.is_equal).then_inc(small, 1)
            dve.wait_ge(small, 1)
            dve.wait_ge(tables, 2)
            dve.scalar_tensor_tensor(out=end_f, in0=same_f, scalar=float(N), in1=dst_f, op0=ALU.mult, op1=ALU.add).then_inc(tables, 1)
            dve.tensor_tensor(keep_b, dst_i, prv_i, ALU.is_equal).then_inc(tables, 1)
            dve.tensor_scalar(gate_b, same_f, 2 * BIG, -BIG, ALU.mult, ALU.add).then_inc(tables, 1)
            for n, first in ((SRC, 0), (DST, 0), (END, BEHIND)):
                dve.wait_ge(idx_turned, n + 1)
                for h in range(HALVES):
                    last = dve.tensor_copy(idx_all[0:ROWS, first:first + EC, n, h::HALVES],
                                           banks[n][0:ROWS, h * NPART:(h + 1) * NPART].rearrange("r (k t) -> r k t", k=EC))
                last.then_inc(idx_ready, 1)
            d0 = dst_f[:, 0:EROWS:ROWS]
            quot, quot_f, rest, low, high, first_f, first_node = (t[:, :] for t in tcol)
            def link(ins, n):
                ins.then_inc(first_step, 1)
                dve.wait_ge(first_step, n)
            link(dve.tensor_scalar(quot, d0, 1.0 / NPART, 0.5 / NPART - 0.5, ALU.mult, ALU.add), 1)
            link(dve.tensor_copy(tcol_i[0][:, :], quot), 2)
            link(dve.tensor_copy(quot_f, tcol_i[0][:, :]), 3)
            link(dve.scalar_tensor_tensor(out=rest, in0=quot_f, scalar=-float(NPART), in1=d0, op0=ALU.mult, op1=ALU.add), 4)
            link(dve.tensor_scalar(low, rest, 0.0, None, ALU.is_lt), 5)
            link(dve.tensor_scalar(high, rest, float(NPART), None, ALU.is_ge), 6)
            link(dve.tensor_tensor(first_f, quot_f, low, ALU.subtract), 7)
            link(dve.tensor_tensor(first_f, first_f, high, ALU.add), 8)
            link(dve.tensor_scalar(first_f, first_f, float(PER_PART - WINDOW), None, ALU.min), 9)
            dve.tensor_copy(tcol_i[1][:, :], first_f).then_inc(rel_ready, 1)
            link(dve.tensor_scalar(first_node, first_f, float(NPART), None, ALU.mult), 10)
            dve.tensor_tensor(rel_f.rearrange("p (h r) -> p h r", h=HALVES), dst_f.rearrange("p (h r) -> p h r", h=HALVES),
                              first_node.unsqueeze(2).to_broadcast([NPART, HALVES, ROWS]), ALU.subtract).then_inc(rel_ready, 1)
            dve.wait_ge(rel_ready, 2)
            dve.tensor_copy(rel_h, rel_f).then_inc(rel_ready, 1)
            dve.tensor_reduce(rel_max[:, :], rel_f, mybir.AxisListType.X, ALU.max).then_inc(rel_ready, 1)
            dve.wait_ge(win_ready, 1)
            dve.tensor_copy(win_f[:, :], win_i[:, :]).then_inc(rel_ready, 1)
            dve.wait_ge(max_turned, 1)
            dve.tensor_reduce(flag_f[:, :], banks[4][0:1, 0:NPART], mybir.AxisListType.X, ALU.max).then_inc(flag_step, 1)
            dve.wait_ge(flag_step, 1)
            dve.tensor_scalar(flag[:, :], flag_f[:, :], float(WINDOW * NPART), None, ALU.is_lt).then_inc(flag_step, 1)
            dve.wait_ge(idx_turned, 4)
            dve.tensor_copy(w_fcT[:, :], banks[3][:, 0:P]).then_inc(idx_ready, 1)
            dve.wait_ge(consts, 16 * N_CONSTS)
            dve.tensor_copy(w2_wide[:, :], w2_col[:, 0:1].to_broadcast([P, P])).then_inc(idx_ready, 1)
            dve.wait_ge(max_turned, 2)
            dve.tensor_copy(snorm_sb[:, :].rearrange("p (q h) -> p h q", h=HALVES),
                            banks[5][0:NPART, 0:PER_PART].rearrange("p (h q) -> p h q", h=HALVES)).then_inc(snorm_ready, 1)
            dve.wait_ge(rel_ready, 5)
            dve.wait_ge(snorm_ready, 1)
            dve.wait_ge(flag_step, 2)
            dve.wait_ge(gates_stored, 48)
            dve.wait_ge(idx_ready, 5)
            dve.memset(gmax[:, 0:1], -BIG).then_inc(carry_ready, 1)
            dve.memset(carry[:, :], 0.0).then_inc(sums_carried, 1)

            def make_onehot(L, narrow):
                def stage(k, u, i):
                    if not narrow:
                        return
                    dve.wait_ge(L["rel"][u], loads_done(i))
                    if gathers_dst(L, k, narrow):
                        dve.nop(nofuse=True).then_inc(L["onehot"], 2)
                        return
                    for half in range(2):
                        if later(k, 2 - half):
                            dve.wait_ge(L["window_used"], (2 * k + half - HSLOTS + 1) * (TPC // 2))
                        dve.tensor_tensor(onehot[(2 * u + half) % HSLOTS],
                                          rel_t[u][:, half * HALF_CHUNK:(half + 1) * HALF_CHUNK].unsqueeze(1).to_broadcast([NPART, WINDOW, HALF_CHUNK]),
                                          win_f[:, :].unsqueeze(2).to_broadcast([NPART, WINDOW, HALF_CHUNK]), ALU.is_equal).then_inc(L["onehot"], 1)
                return stage

            def running_max0(k, u, i):
                dve.wait_ge(L0["zs_copied"], k + 1)
                if later(k, 1):
                    dve.wait_ge(num_ready, k)
                dve.tensor_tensor(e_t, banks[3][:, 0:CHUNK], zsT, ALU.mult).then_inc(e_ready, 1)
                if later(k, 1):
                    dve.wait_ge(gmax_ready, k)
                    dve.tensor_copy(gmax[:, 0:1], gmax[:, CHUNK:CHUNK + 1]).then_inc(carry_ready, 1)
                dve.wait_ge(e_ready, k + 1)
                dve.wait_ge(carry_ready, k + 1)
                dve.wait_ge(L0["gates"][u], loads_done(i))
                dve.tensor_tensor_scan(gmax[:, 1:CHUNK + 1], e_t, gate_t[u][:, 0:CHUNK], gmax[:, 0:1], ALU.max, ALU.min).then_inc(gmax_ready, 1)
                dve.wait_ge(gmax_ready, k + 1)
                dve.tensor_tensor(delta, e_t, gmax[:, 0:CHUNK], ALU.subtract).then_inc(delta_ready, 1)

            def sums0(k, u, i):
                dve.wait_ge(exps_ready, k + 1)
                dve.tensor_tensor(e_t, ex_t, zsT, ALU.mult).then_inc(w_ready, 1)
                if later(k, 1):
                    dve.wait_ge(num_ready, k)
                    dve.tensor_copy(carry[:, 0:1], den[:, CHUNK - 1:CHUNK])
                    dve.tensor_copy(carry[:, 1:2], num[:, CHUNK - 1:CHUNK]).then_inc(sums_carried, 1)
                    dve.wait_ge(L0["y_ready"], k)
                dve.wait_ge(sums_carried, k + 1)
                dve.tensor_tensor_scan(den, c_t, ex_t, carry[:, 0:1], ALU.mult, ALU.add).then_inc(den_ready, 1)
                dve.wait_ge(w_ready, k + 1)
                dve.tensor_tensor_scan(num, c_t, e_t, carry[:, 1:2], ALU.mult, ALU.add).then_inc(num_ready, 1)

            def divide0(k, u, i):
                dve.wait_ge(rec_ready, k + 1)
                if later(k, 1):
                    dve.wait_ge(L0["y_turned"], k)
                dve.wait_ge(num_ready, k + 1)
                dve.tensor_tensor(y_t, num, rec_t, ALU.mult).then_inc(L0["y_ready"], 1)
            by_width(dve, lambda narrow: pipeline(dve, EC, ESLOTS, (2, running_max0), (3, divide0), (0, make_onehot(L0, narrow)), (2, sums0)))

            HALF = TPN * NPART // 2
            def stats(c, u, i):
                dve.wait_ge(kept, c + 1)
                for h in range(2):
                    last = dve.bn_stats(st0[:, bass.ds(2 * c + h, 1), :].rearrange("p o s -> p (o s)"),
                                        node_table[:, bass.ds(c * CW + h * HALF, HALF)])
                last.then_inc(stats0, 1)

            def scale_rows(c, u, i):
                dve.wait_ge(hout_loaded[u], loads_done(i))
                if later(c, NSLOTS):
                    dve.wait_ge(node_turned, c - NSLOTS + 1)
                dve.tensor_tensor(nv[u][:, 0:DVE_ROWS, :], nx[u][:, 0:DVE_ROWS, :],
                                  snorm_sb[:, bass.ds(c * TPN, DVE_ROWS)].unsqueeze(2).to_broadcast([NPART, DVE_ROWS, D]), ALU.mult).then_inc(scaled, 1)
            pipeline(dve, NCH, NSLOTS, (0, scale_rows), (2, stats))
            dve.wait_ge(stats0, NCH)
            dve.bn_aggr(mv0, st0[:, :, :].rearrange("p c s -> p (c s)")).then_inc(bn_step, 1)
            dve.wait_ge(bn_root, 1)
            dve.tensor_tensor(a_col, g0_col, rs_col, ALU.mult).then_inc(bn_step, 1)
            dve.wait_ge(bn_step, 2)
            dve.tensor_tensor(ma_col, mv0[:, 0:1], a_col, ALU.mult).then_inc(bn_step, 1)
            dve.wait_ge(bn_step, 3)
            dve.tensor_tensor(b_col, be0_col, ma_col, ALU.subtract).then_inc(bn_step, 1)
            dve.wait_ge(bn_step, 4)
            dve.tensor_scalar(na_col, a_col, -1.0, None, ALU.mult).then_inc(bn_step, 1)
            dve.tensor_scalar(nb_col, b_col, -1.0, None, ALU.mult).then_inc(bn_step, 1)
            dve.wait_ge(kept, NCH)

            def row_stats(rows, st, c, u, st_sem):
                dve.nop(nofuse=True)
                for j in range(TPN):
                    last = dve.bn_stats(st[:, u, j, :], rows[j])
                last.then_inc(st_sem, 1)
            def row_moments(st, mv, st_sem, mv_sem, used):
                def stage(c, u, i):
                    dve.wait_ge(st_sem, c + 1)
                    if later(c, NSLOTS):
                        dve.wait_ge(used, c - NSLOTS + 1)
                    dve.nop(nofuse=True)
                    for j in range(TPN):
                        last = dve.bn_aggr(mv[:, u, j, :], st[:, u, j, :])
                    last.then_inc(mv_sem, 1)
                return stage

            def shift(mv, rs, mb, rs_sem, mb_sem):
                def stage(c, u, i):
                    dve.wait_ge(rs_sem, c + 1)
                    dve.scalar_tensor_tensor(out=mb[:, u, :], in0=mv[:, u, :, 0:1].rearrange("p j o -> p (j o)"), scalar=-1.0,
                                             in1=rs[:, u, :], op0=ALU.mult, op1=ALU.mult).then_inc(mb_sem, 1)
                return stage

            def residual(c, u, i):
                dve.wait_ge(elu_turned, c + 1)
                dve.wait_ge(x_loaded[u], loads_done(i))
                pair = BANK_PAIR[u]
                dve.scalar_tensor_tensor(out=node_rows(c), in0=psum[0:NPART, pair * 512:pair * 512 + CW].rearrange("p (j f) -> p j f", f=D),
                                         scalar=-1.0, in1=nx[u], op0=ALU.add, op1=ALU.add).then_inc(s_ready, 1)
            def norm_rows(c, u, i):
                dve.wait_ge(n1["mb"], c + 1)
                for j in range(ACT_NORM_FROM):
                    row = node_row(c, j)
                    a = dve.tensor_scalar(row, row, rsA[:, u, j:j + 1], mbA[:, u, j:j + 1], ALU.mult, ALU.add)
                a.then_inc(norm_dve, 1)
            def residual_stats(c, u, i):
                dve.wait_ge(s_ready, c + 1)
                row_stats([node_row(c, j) for j in range(TPN)], stA, c, u, n1["st"])
            pipeline(dve, NCH, NSLOTS, (1, row_moments(stA, mvA, n1["st"], n1["mv"], norm_act)), (3, shift(mvA, rsA, mbA, n1["rs"], n1["mb"])),
                     (0, residual), (3, norm_rows), (0, residual_stats))

            def step1(k, u, i):
                dve.wait_ge(L1["weight"], k + 1)
                if later(k, 1):
                    dve.wait_ge(L1["y_ready"], k)
                dve.tensor_tensor(msg, att_w, xsT, ALU.mult).then_inc(msg_ready, 1)
                dve.wait_ge(msg_ready, k + 1)
                dve.wait_ge(L1["gates"][u], loads_done(i))
                if later(k, ESLOTS):
                    dve.wait_ge(L1["y_turned"], k - ESLOTS + 1)
                dve.tensor_tensor_scan(aggT[u], gate_t[u][:, 0:CHUNK], msg,
                                       0.0 if not later(k, 1) else aggT[(u - 1) % ESLOTS][:, CHUNK - 1:CHUNK], ALU.mult, ALU.add).then_inc(L1["y_ready"], 1)
            by_width(dve, lambda narrow: pipeline(dve, EC, ESLOTS, (0, make_onehot(L1, narrow)), (2, step1)))

            def stats_a(c, u, i):
                dve.wait_ge(n2["att"], c + 1)
                row_stats([nx[u][:, j, :] for j in range(TPN)], stA, c, u, n2["stA"])
            def gamma_rest(c, u, i):
                dve.wait_ge(n2["normA"], c + 1)
                dve.tensor_tensor(nv[u][:, GAMMA_ROWS:TPN, :], nv[u][:, GAMMA_ROWS:TPN, :],
                                  g1_row[:, :].unsqueeze(1).to_broadcast([NPART, TPN - GAMMA_ROWS, D]), ALU.mult).then_inc(n2["t_rest"], 1)
            def add_xb(c, u, i):
                dve.wait_ge(n2["xb"], c + 1)
                dve.wait_ge(n2["t"], c + 1)
                dve.wait_ge(n2["t_rest"], c + 1)
                dve.tensor_tensor(nv[u], nv[u], ne[u], ALU.add).then_inc(n2["s"], 1)
            def stats_b(c, u, i):
                dve.wait_ge(n2["s"], c + 1)
                row_stats([nv[u][:, j, :] for j in range(TPN)], stB, c, u, n2["stB"])
            def norm_b_rest(c, u, i):
                dve.wait_ge(n2["mbB"], c + 1)
                if later(c, NSLOTS):
                    dve.wait_ge(out_stored[u], 16 * i)
                for j in range(OUT_ROWS, TPN):
                    last = dve.tensor_scalar(no[u][:, j, :], nv[u][:, j, :], rsB[:, u, j:j + 1], mbB[:, u, j:j + 1], ALU.mult, ALU.add)
                last.then_inc(n2["normB_rest"], 1)
            def inverse(sd, sd_sem, rs_sem):
                def stage(c, u, i):
                    dve.wait_ge(sd_sem, c + 1)
                    dve.reciprocal(sd[:, u, :], sd[:, u, :]).then_inc(rs_sem, 1)
                return stage
            pipeline(dve, NCH, NSLOTS, (4, row_moments(stB, mvB, n2["stB"], n2["mvB"], n2["normB"])), (3, gamma_rest), (0, stats_a),
                     (1, inverse(rsA, n2["sdA"], n2["rsA"])), (5, inverse(rsB, n2["sdB"], n2["rsB"])), (3, add_xb), (0, row_moments(stA, mvA, n2["stA"], n2["mvA"], n2["normA"])), (1, shift(mvA, rsA, mbA, n2["rsA"], n2["mbA"])),
                     (5, shift(mvB, rsB, mbB, n2["rsB"], n2["mbB"])), (3, stats_b), (5, norm_b_rest))


_INS = ["x", "src", "dst", "node_vec1", "L0_gnn_W_fc", "L0_gnn_gamma", "L0_gnn_beta", "L1_gnn_W1", "L1_gnn_b1",
        "L1_gnn_W2", "L1_gnn_b2", "L1_gnn_gamma", "L1_gnn_beta"]


def kernel(**inputs):
    import numpy as _np
    import concourse.bacc as _bacc
    from concourse import mybir as _mybir
    from concourse.bass_utils import run_bass_kernel_spmd as _run

    nc = _bacc.Bacc("TRN2", target_bir_lowering=False, num_devices=1)
    arrays, args = {}, []
    for name in _INS:
        a = _np.ascontiguousarray(inputs[name])
        arrays[f"in_{name}"] = a
        args.append(nc.dram_tensor(f"in_{name}", a.shape, _mybir.dt.from_np(a.dtype), kind="ExternalInput").ap())
    out = nc.dram_tensor("out_0", inputs["x"].shape, _mybir.dt.float32, kind="ExternalOutput").ap()
    gnn_two_layers(nc, *args, out)
    r = _run(nc, [arrays], core_ids=[0])
    return r.results[0]["out_0"]
```
